# Optimizing a Trainium2 kernel written in Bass

```python
import numpy as np
import jax
import jax.numpy as jnp

def _softmax(x, axis=-1):
    return jax.nn.softmax(x, axis=axis)

def _gelu(x):
    return jax.nn.gelu(x, approximate=True)

def _silu(x):
    return jax.nn.silu(x)

def _sigmoid(x):
    return jax.nn.sigmoid(x)

def _layernorm(x, axis=-1, eps=1e-05):
    m = jnp.mean(x, axis=axis, keepdims=True)
    v = jnp.var(x, axis=axis, keepdims=True)
    return (x - m) / jnp.sqrt(v + eps)

def _scatter_add(tgt, idx, src, axis=0):
    return tgt.at[idx].add(src)

def _segment_sum(src, seg, n):
    return jax.ops.segment_sum(src, seg, n)
kernel_name = 'mk_prb_d1_jaxref_r8_f9694c'

def setup_inputs(seed: int=0):
    np.random.seed(seed)
    _w = jnp.asarray

    def _L0_attn_setup():
        import jax, jax.numpy as jnp
        import numpy as np
        B, S, DIM, H, DH = (1, 1024, 256, 32, 64)
        W = 128
        CBS = 64
        NMEM = 4
        SCALE = DH ** (-0.5)

        def rms_norm(x, w):
            eps = jnp.finfo(x.dtype).eps
            return x * jax.lax.rsqrt(jnp.mean(x * x, axis=-1, keepdims=True) + eps) * w

        def local_attention(q, k, v):
            b, h, n, d = q.shape
            nb = n // W
            qb = q.reshape(b, h, nb, W, d)
            kb = k.reshape(b, h, nb, W, d)
            vb = v.reshape(b, h, nb, W, d)
            prev = lambda t: jnp.concatenate([jnp.zeros_like(t[:, :, :1]), t[:, :, :-1]], axis=2)
            kk = jnp.concatenate([prev(kb), kb], axis=3)
            vv = jnp.concatenate([prev(vb), vb], axis=3)
            sim = jnp.einsum('bhnid,bhnjd->bhnij', qb, kk) * SCALE
            qi = jnp.arange(nb)[:, None] * W + jnp.arange(W)[None, :]
            kj = (jnp.arange(nb)[:, None] - 1) * W + jnp.arange(2 * W)[None, :]
            dist = qi[:, :, None] - kj[:, None, :]
            allowed = (dist >= 0) & (dist <= W) & (kj[:, None, :] >= 0)
            sim = jnp.where(allowed[None, None], sim, -jnp.finfo(sim.dtype).max)
            attn = jax.nn.softmax(sim, axis=-1)
            out = jnp.einsum('bhnij,bhnjd->bhnid', attn, vv)
            return out.reshape(b, h, n, d)
        key = jax.random.key(seed)
        ks = jax.random.split(key, 12)
        di = H * DH
        f = lambda k, shape: jax.random.normal(k, shape, jnp.float32) * 0.02
        return dict(inp=jax.random.normal(ks[0], (B, S, DIM), jnp.float32), rms_w=jnp.ones((DIM,), jnp.float32), w_qkv=f(ks[1], (DIM, 3 * di)), k_pos=f(ks[2], (H, CBS, DH)), v_pos=f(ks[3], (H, CBS, DH)), kc_w=f(ks[4], (H, DH, DH, CBS)), kc_b=f(ks[5], (H, DH)), vc_w=f(ks[6], (H, DH, DH, CBS)), vc_b=f(ks[7], (H, DH)), mem_kv=f(ks[8], (2, H, NMEM, DH)), w_comb=f(ks[9], (DIM, 3 * H)), b_comb=jnp.zeros((3 * H,), jnp.float32), w_out=f(ks[10], (di, DIM)))
    _L0_attn_in = _L0_attn_setup()

    def _L0_ffn_setup():
        import jax, jax.numpy as jnp
        import numpy as np
        EPS = 1e-08

        def _bit_quant(w):
            scale = jnp.maximum(jnp.mean(jnp.abs(w)), EPS)
            w_ternary = jnp.clip(jnp.round(w / scale), -1.0, 1.0)
            return w + jax.lax.stop_gradient(w_ternary - w)
        key = jax.random.key(seed)
        k = jax.random.split(key, 5)
        emb, dff = (256, 1024)
        B, S = (4, 256)
        x = jax.random.normal(k[0], (B, S, emb), dtype=jnp.float32)
        w1 = jax.random.normal(k[1], (dff, emb), dtype=jnp.float32) * 0.02
        b1 = jax.random.normal(k[2], (dff,), dtype=jnp.float32) * 0.02
        w2 = jax.random.normal(k[3], (emb, dff), dtype=jnp.float32) * 0.02
        b2 = jax.random.normal(k[4], (emb,), dtype=jnp.float32) * 0.02
        return {'x': x, 'w1': w1, 'b1': b1, 'w2': w2, 'b2': b2}
    _L0_ffn_in = _L0_ffn_setup()
    _d = {'L0_attn_inp': _L0_attn_in['inp'], 'L0_attn_rms_w': _L0_attn_in['rms_w'], 'L0_attn_w_qkv': _L0_attn_in['w_qkv'], 'L0_attn_k_pos': _L0_attn_in['k_pos'], 'L0_attn_v_pos': _L0_attn_in['v_pos'], 'L0_attn_kc_w': _L0_attn_in['kc_w'], 'L0_attn_kc_b': _L0_attn_in['kc_b'], 'L0_attn_vc_w': _L0_attn_in['vc_w'], 'L0_attn_vc_b': _L0_attn_in['vc_b'], 'L0_attn_mem_kv': _L0_attn_in['mem_kv'], 'L0_attn_w_comb': _L0_attn_in['w_comb'], 'L0_attn_b_comb': _L0_attn_in['b_comb'], 'L0_attn_w_out': _L0_attn_in['w_out'], 'L0_ffn_w1': _L0_ffn_in['w1'], 'L0_ffn_b1': _L0_ffn_in['b1'], 'L0_ffn_w2': _L0_ffn_in['w2'], 'L0_ffn_b2': _L0_ffn_in['b2']}
    _x0 = _d['L0_attn_inp']
    _d['L0_attn_inp'] = jax.random.normal(jax.random.fold_in(jax.random.key(seed), 1), (1, 1024, 256), dtype=_x0.dtype)
    del _x0
    return _d

def reference(L0_attn_inp, L0_attn_rms_w, L0_attn_w_qkv, L0_attn_k_pos, L0_attn_v_pos, L0_attn_kc_w, L0_attn_kc_b, L0_attn_vc_w, L0_attn_vc_b, L0_attn_mem_kv, L0_attn_w_comb, L0_attn_b_comb, L0_attn_w_out, L0_ffn_w1, L0_ffn_b1, L0_ffn_w2, L0_ffn_b2):

    def _L0_attn_ref(inp, rms_w, w_qkv, k_pos, v_pos, kc_w, kc_b, vc_w, vc_b, mem_kv, w_comb, b_comb, w_out):
        import jax, jax.numpy as jnp
        import numpy as np
        B, S, DIM, H, DH = (1, 1024, 256, 32, 64)
        W = 128
        CBS = 64
        NMEM = 4
        SCALE = DH ** (-0.5)

        def rms_norm(x, w):
            eps = jnp.finfo(x.dtype).eps
            return x * jax.lax.rsqrt(jnp.mean(x * x, axis=-1, keepdims=True) + eps) * w

        def local_attention(q, k, v):
            b, h, n, d = q.shape
            nb = n // W
            qb = q.reshape(b, h, nb, W, d)
            kb = k.reshape(b, h, nb, W, d)
            vb = v.reshape(b, h, nb, W, d)
            prev = lambda t: jnp.concatenate([jnp.zeros_like(t[:, :, :1]), t[:, :, :-1]], axis=2)
            kk = jnp.concatenate([prev(kb), kb], axis=3)
            vv = jnp.concatenate([prev(vb), vb], axis=3)
            sim = jnp.einsum('bhnid,bhnjd->bhnij', qb, kk) * SCALE
            qi = jnp.arange(nb)[:, None] * W + jnp.arange(W)[None, :]
            kj = (jnp.arange(nb)[:, None] - 1) * W + jnp.arange(2 * W)[None, :]
            dist = qi[:, :, None] - kj[:, None, :]
            allowed = (dist >= 0) & (dist <= W) & (kj[:, None, :] >= 0)
            sim = jnp.where(allowed[None, None], sim, -jnp.finfo(sim.dtype).max)
            attn = jax.nn.softmax(sim, axis=-1)
            out = jnp.einsum('bhnij,bhnjd->bhnid', attn, vv)
            return out.reshape(b, h, n, d)
        b, n, _ = inp.shape
        x = rms_norm(inp, rms_w)
        q, k, v = jnp.split(x @ w_qkv, 3, axis=-1)
        split = lambda t: t.reshape(b, n, H, DH).transpose(0, 2, 1, 3)
        q, k, v = (split(q), split(k), split(v))
        nc = n // CBS
        kb = (k + jnp.tile(k_pos, (1, nc, 1))).reshape(b, H, nc, CBS, DH)
        vb = (v + jnp.tile(v_pos, (1, nc, 1))).reshape(b, H, nc, CBS, DH)
        ck = jnp.einsum('bhnti,hoit->bhno', kb, kc_w) + kc_b[None, :, None, :]
        cv = jnp.einsum('bhnti,hoit->bhno', vb, vc_w) + vc_b[None, :, None, :]
        ck = jnp.concatenate([jnp.broadcast_to(mem_kv[0], (b, H, NMEM, DH)), ck], axis=2)
        cv = jnp.concatenate([jnp.broadcast_to(mem_kv[1], (b, H, NMEM, DH)), cv], axis=2)
        csim = jnp.einsum('bhid,bhjd->bhij', q, ck) * SCALE
        cq_seq = jnp.arange(n)
        ck_seq = (jnp.arange(nc) + 1) * CBS - 1
        ck_seq = jnp.concatenate([jnp.full((NMEM,), -1, ck_seq.dtype), ck_seq])
        cmask = ck_seq[None, :] < cq_seq[:, None]
        csim = jnp.where(cmask[None, None], -jnp.finfo(csim.dtype).max, csim)
        cattn = jax.nn.softmax(csim, axis=-1)
        comp = jnp.einsum('bhij,bhjd->bhid', cattn, cv)
        local = local_attention(q, k, v)
        cw = jax.nn.sigmoid(x @ w_comb + b_comb).reshape(b, n, H, 3).transpose(0, 2, 1, 3)
        out = (cw[..., 0:1] + cw[..., 1:2]) * local + cw[..., 2:3] * comp
        out = out.transpose(0, 2, 1, 3).reshape(b, n, H * DH)
        return out @ w_out

    def _L0_ffn_ref(x, w1, b1, w2, b2):
        import jax, jax.numpy as jnp
        import numpy as np
        EPS = 1e-08

        def _bit_quant(w):
            scale = jnp.maximum(jnp.mean(jnp.abs(w)), EPS)
            w_ternary = jnp.clip(jnp.round(w / scale), -1.0, 1.0)
            return w + jax.lax.stop_gradient(w_ternary - w)
        w1q = _bit_quant(w1)
        w2q = _bit_quant(w2)
        h = jnp.einsum('bsd,fd->bsf', x, w1q) + b1
        h = jax.nn.gelu(h, approximate=False)
        return jnp.einsum('bsf,df->bsd', h, w2q) + b2
    x = L0_attn_inp
    xn = _layernorm(x, axis=-1)
    x = x + _L0_attn_ref(xn, L0_attn_rms_w, L0_attn_w_qkv, L0_attn_k_pos, L0_attn_v_pos, L0_attn_kc_w, L0_attn_kc_b, L0_attn_vc_w, L0_attn_vc_b, L0_attn_mem_kv, L0_attn_w_comb, L0_attn_b_comb, L0_attn_w_out) + _L0_ffn_ref(xn, L0_ffn_w1, L0_ffn_b1, L0_ffn_w2, L0_ffn_b2)
    return x

_drawn_inputs = setup_inputs


def setup_inputs(seed=0):
    import zlib

    import numpy as np

    out = dict(_drawn_inputs(seed))
    spreads = {'L0_attn_rms_w': (1.0, 0.6), 'L0_attn_b_comb': (0.0, 0.8)}
    factors = {'L0_attn_w_qkv': 8.0,
     'L0_attn_k_pos': 200.0,
     'L0_attn_v_pos': 8.0,
     'L0_attn_kc_w': 8.0,
     'L0_attn_kc_b': 200.0,
     'L0_attn_vc_w': 8.0,
     'L0_attn_vc_b': 200.0,
     'L0_attn_w_comb': 8.0,
     'L0_attn_w_out': 8.0,
     'L0_ffn_b1': 50.427,
     'L0_ffn_b2': 200.0}
    for name, (base, spread) in spreads.items():
        noise = np.random.default_rng([zlib.crc32(name.encode()), seed]).standard_normal(out[name].shape)
        drawn = base * np.exp(spread * noise) if base else spread * noise
        out[name] = jnp.asarray(drawn.astype(out[name].dtype))
    for name, factor in factors.items():
        out[name] = (out[name] * factor).astype(out[name].dtype)
    return out
```

```python
from contextlib import ExitStack

import concourse.bass as bass
from concourse import mybir

F32 = mybir.dt.float32
ALU = mybir.AluOpType
ACT = mybir.ActivationFunctionType
AX = mybir.AxisListType

P = 128
S, DIM, H, DH = 1024, 256, 32, 64
W = 128
CBS = 64
NB = S // CBS
T = S // P
KT = DIM // P
NP = H // 2
DFF = 1024
FT = DFF // P
SCALE = DH ** -0.5
NEG = -1e30
LN_EPS, RMS_EPS, Q_EPS = 1e-5, 1.1920929e-07, 1e-8
ROUND = 1.5 * 2 ** 23

PRO_ITEMS = [f"{n}{j}" for n in ("xr", "xn", "pos", "w1", "w2") for j in range(4)] + ["g0", "g1"]
PREP0 = ["k0", "k1", "v0", "v1", "q0", "q1", "t0", "t1"]
FFN_ITEMS = [f"h{g}_{f}" for g in range(2) for f in range(FT)]
FFN_OUT = [f"f{g}_{j}" for g in range(2) for j in range(2)]
ORDER = PRO_ITEMS + PREP0 + [x for g in range(2) for x in FFN_ITEMS[g * FT:(g + 1) * FT] + FFN_OUT[g * 2:g * 2 + 2]]
RING0 = len(ORDER)
PAIR_ITEMS = ["k0", "k1", "v0", "v1", "q0", "q1", "c0", "c1", "t0", "t1"]
RING_PER_PAIR = len(PAIR_ITEMS)
assert RING0 % 2 == 0 and all(int(x[-1]) % 2 == n % 2 for n, x in enumerate(ORDER))


def layer(nc, inp, rms_w, w_qkv, k_pos, v_pos, kc_w, kc_b, vc_w, vc_b, w_comb, b_comb, w_out,
          w1, b1, w2, b2, out):
    with ExitStack() as ctx:
        def sb(name, shape):
            return ctx.enter_context(nc.sbuf_tensor(name, shape, F32))

        def sem(name):
            return ctx.enter_context(nc.semaphore(name))

        acc = sb("acc", [P, T, DIM])
        xr_T = sb("xr_T", [P, KT, S])
        pos_T = sb("pos_T", [P, NP, 2, CBS])
        conv_w = [sb(f"conv_w{s}", [P, 2, DH, CBS]) for s in range(2)]
        proj_w = [sb(f"proj_w{s}", [P, KT, 3, P]) for s in range(2)]
        out_w = [sb(f"out_w{s}", [P, DIM]) for s in range(2)]
        conv_b = [sb(f"conv_b{s}", [P, P]) for s in range(2)]
        kz = [[sb(f"kz{s}{h}", [P, S]) for h in range(2)] for s in range(2)]
        q_T = [sb(f"q_T{s}", [P, S]) for s in range(2)]
        v_T = sb("v_T", [P, S])
        v_tok = [sb(f"v_tok{s}", [P, T, P]) for s in range(2)]
        kvb = sb("kvb", [P, CBS, 64])
        s_neg = sb("s_neg", [P, 2, 2, 2 * W])
        prob = sb("prob", [P, 4, 2, 2 * W])
        prob_T = sb("prob_T", [P, 2, 4, P])
        o_T = sb("o_T", [P, 2, 4 * P])
        ncol = sb("ncol", [P, T, 2])
        lsum = sb("lsum", [P, T, 2])
        rinv = sb("rinv", [P, T, 2])
        rloc = sb("rloc", [P, T, 2])
        gate_p = sb("gate_p", [P, 2, T, 2])
        gate = sb("gate", [P, NP, 2, T, 2])
        c_s = sb("c_s", [P, T, 2, NB])
        c_e = sb("c_e", [P, T, 2, NB])
        c_p = sb("c_p", [P, T, 2, NB])
        c_m = sb("c_m", [P, T * 2])
        c_l = sb("c_l", [P, T * 2])
        c_r = sb("c_r", [P, T * 2])
        c_g = sb("c_g", [P, T * 2])
        pc_T = sb("pc_T", [P, S])
        conv_s = sb("conv_s", [P, P])
        ck_bd = sb("ck_bd", [P, 2 * NB])
        cv_bd = sb("cv_bd", [P, P])
        ident = sb("ident", [P, P])
        sel = sb("sel", [P, 64])
        ones = sb("ones", [P, P])
        mask_l = sb("mask_l", [P, 2, W])
        mask_c = sb("mask_c", [P, T, NB])
        block_m = sb("block_m", [32, 2, DH])
        rms_c = sb("rms_c", [P, KT])
        b1_c = sb("b1_c", [P, FT])
        b2_r = sb("b2_r", [P, DIM])
        bc_r = sb("bc_r", [P, 3 * H])
        wcomb = sb("wcomb", [P, KT, 3 * H])
        stat = sb("stat", [P, 8, T])
        wstat = sb("wstat", [P, 8])
        sig = sb("sig", [P, T, 3 * H])
        xc = sb("xc", [P, T, DIM])
        xn_T = sb("xn_T", [P, KT, S])
        w1_s = kvb[:].rearrange("p a b -> p (a b)")[:, 0:2048].rearrange("p (j c) -> p j c", j=FT)
        w2_s = kvb[:].rearrange("p a b -> p (a b)")[:, 2048:4096].rearrange("p (j f) -> p j f", j=2)
        big = conv_w[1][:].rearrange("p a b c -> p (a b c)")
        h_T = big[:, 0:4096].rearrange("p (f n) -> p f n", f=FT)
        w1_T = big[:, 4096:6144].rearrange("p (k f) -> p k f", k=KT)
        w2_T = big[:, 6144:8192].rearrange("p (f e) -> p f e", f=FT)
        xsq = prob[:].rearrange("p a b c -> p (a b c)").rearrange("p (b c) -> p b c", b=T)
        pos_raw = xsq.rearrange("p a b -> p (a b)").rearrange("p (h d) -> p h d", h=H)

        bank = [ctx.enter_context(nc.psum_tensor(f"bank{n}", [P, 512], F32)) for n in range(8)]
        ring, p_conv, p_sim, p_pt, p_o, p_y = bank[0:2], bank[2], bank[3:5], bank[5], bank[6], bank[7]
        ck_ps = p_conv[:, 128:160]
        cv_ps = p_conv[0:32, 192:256]
        csim_ps = p_conv[:, 256:512].rearrange("p (b h n) -> p b h n", b=T, h=2)

        x_in, small_in, w12_in, pos_in = sem("x_in"), sem("small_in"), sem("w12_in"), sem("pos_in")
        proj_in = [sem(f"proj_in{s}") for s in range(2)]
        conv_in = [sem(f"conv_in{s}") for s in range(2)]
        bias_in = [sem(f"bias_in{s}") for s in range(2)]
        outw_in = [sem(f"outw_in{s}") for s in range(2)]
        consts = sem("consts")
        zeroed = sem("zeroed")
        ln = sem("ln")
        rt_in, rt_out = sem("rt_in"), sem("rt_out")
        dch = sem("dch")
        pch = sem("pch")
        wsum, wtot, wq_ready = sem("wsum"), sem("wtot"), sem("wq_ready")
        glog, gexp, gates = sem("glog"), sem("gexp"), sem("gates")
        filled = [sem(f"ring_filled{n}") for n in range(2)]
        emptied = [sem(f"ring_emptied{n}") for n in range(2)]
        bd2_ready, bd_ready, conv_done, conv_evac = sem("bd2_ready"), sem("bd_ready"), sem("conv_done"), sem("conv_evac")
        sel_done, ckcv, csim_done = sem("sel_done"), sem("ckcv"), sem("csim_done")
        csim_read, cs_ready, ce_ready, pc_ready = sem("csim_read"), sem("cs_ready"), sem("ce_ready"), sem("pc_ready")
        cchain, lchain = sem("cchain"), sem("lchain")
        sim_done, sim_read, exp_done = sem("sim_done"), sem("sim_read"), sem("exp_done")
        r_ready, p_ready, pt_done, pt_evac = sem("r_ready"), sem("p_ready"), sem("pt_done"), sem("pt_evac")
        pv_done, o_evac, y_done, y_added = sem("pv_done"), sem("o_evac"), sem("y_done"), sem("y_added")
        step_begun = sem("step_begun")
        stored = sem("stored")

        FREE_SIM, FREE_EXP, FREE_PT, FREE_PV, FREE_Y, FREE_BANK = 2, 4, 4, 2, 3, 1

        def wait_filled(eng, k):
            eng.wait_ge(filled[k % 2], k // 2 + 1)

        def pro(name):
            return ORDER.index(name)

        class Pair:

            def __init__(self, i, s):
                self.i, self.s, self.p = i, s, i * 2 + s
                self.nxt = None if s == -1 else (1 - s)
                self.nxt_use = i + s

            def ordinal_last(self, name):
                return self.p * (RING_PER_PAIR // 2) + (RING0 // 2 + 1)

            def ordinal(self, name):
                return self.p * (RING_PER_PAIR // 2) + (RING0 // 2 + PAIR_ITEMS.index(name) // 2 + 1)

        def ring_wait_free(pe, b, ordinal):
            pe.wait_ge(emptied[b], ordinal - 1)

        block = ctx.enter_context(nc.Block())

        @block.sync
        def _(sp):
            def load_proj(q, s):
                for kt in range(KT):
                    sp.dma_start(proj_w[s][:, kt], w_qkv[kt * P:(kt + 1) * P].rearrange("c (j n) -> c j n", j=3)[:, :, bass.ds(q * P, P)]).then_inc(proj_in[s], 16)

            def load_conv(q, s):
                for kv, src in enumerate((kc_w, vc_w)):
                    for h in range(2):
                        sp.dma_start(conv_w[s][64 * h:64 * h + 64, kv],
                                     src[bass.ds(q * 2 + h, 1)].rearrange("a o i t -> (a i) o t")).then_inc(conv_in[s], 16)

            def load_bias(q, s):
                for kv, src in enumerate((kc_b, vc_b)):
                    for h in range(2):
                        r = 32 * kv + 16 * h
                        sp.dma_start(conv_b[s][r:r + 16, 64 * kv:64 * kv + 64],
                                     src[bass.ds(q * 2 + h, 1)].broadcast_to([16, DH])).then_inc(bias_in[s], 16)

            def load_outw(q, s):
                sp.dma_start(out_w[s][:], w_out[bass.ds(q * P, P)]).then_inc(outw_in[s], 16)

            sp.dma_start(acc[:], inp[0].rearrange("(b p) c -> p b c", p=P)).then_inc(x_in, 16)
            sp.dma_start(rms_c[:], rms_w.rearrange("(k p) -> p k", p=P), allow_slow_non_contiguous=True).then_inc(small_in, 16)
            sp.dma_start(b1_c[:], b1.rearrange("(f p) -> p f", p=P), allow_slow_non_contiguous=True).then_inc(small_in, 16)
            sp.dma_start(b2_r[:], b2.partition_broadcast(P)).then_inc(small_in, 16)
            sp.dma_start(bc_r[:], b_comb.partition_broadcast(P)).then_inc(small_in, 16)
            sp.dma_start(wcomb[:], w_comb.rearrange("(k p) n -> p k n", p=P)).then_inc(small_in, 16)
            sp.dma_start(w1_s, w1.rearrange("(j p) c -> p j c", p=P)).then_inc(w12_in, 16)
            sp.dma_start(w2_s, w2.rearrange("(j p) f -> p j f", p=P)).then_inc(w12_in, 16)
            load_proj(0, 0)
            sp.wait_ge(consts, 1)
            load_bias(0, 0)
            load_conv(0, 0)
            load_outw(0, 0)
            load_proj(1, 1)
            load_bias(1, 1)
            load_outw(1, 1)
            sp.wait_ge(filled[1], pro("xr3") // 2 + 1)
            for n, src in enumerate((k_pos, v_pos)):
                sp.dma_start(pos_raw[64 * n:64 * n + 64], src.rearrange("h t d -> t h d")).then_inc(pos_in, 16)
            sp.wait_ge(filled[1], pro("f1_1") // 2 + 1)
            load_conv(1, 1)

            def pair(i, s):
                p = i * 2 + s
                sp.wait_ge(filled[1], p * (RING_PER_PAIR // 2) + (RING0 // 2 - 2))
                load_proj(p + 2, s)
                sp.wait_ge(conv_evac, p + 1)
                load_conv(p + 2, s)
                load_bias(p + 2, s)
                sp.wait_ge(y_done, p * 4 + (FREE_Y + 4))
                load_outw(p + 2, s)

            with sp.Fori(0, NP // 2 - 1) as i:
                pair(i, 0)
                pair(i, 1)
            for m in range(4):
                sp.wait_ge(y_added, 4 * (NP - 1) + m + 1 + FREE_BANK)
                sp.dma_start(out[0, 256 * m:256 * m + 256].rearrange("(b p) c -> p b c", p=P),
                             acc[:, 2 * m:2 * m + 2]).then_inc(stored, 16)
            sp.wait_ge(stored, 64)

        @block.gpsimd
        def _(pool):
            n = [0]

            def link(ins):
                n[0] += 1
                ins.then_inc(pch, 1)
                pool.wait_ge(pch, n[0])

            for s in range(2):
                link(pool.memset(conv_b[s][:], 0.0))
            link(pool.memset(ident[:], 0.0))
            pool.sem_inc(consts, 1)
            link(pool.memset(ones[:], 1.0))
            link(pool.affine_select(out=ident[:], in_=ident[:], compare_op=ALU.not_equal, fill=1.0, base=0,
                                    pattern=[[-1, P]], channel_multiplier=1))
            link(pool.memset(mask_l[:], 0.0))
            link(pool.memset(mask_c[:], 0.0))
            link(pool.memset(block_m[:], 1.0))
            link(pool.tensor_tensor(out=sel[:], in0=ident[:, 0:64], in1=ident[:, 64:128], op=ALU.add))
            link(pool.affine_select(out=mask_l[:, 0], in_=mask_l[:, 0], compare_op=ALU.is_ge, fill=NEG, base=0,
                                    pattern=[[1, W]], channel_multiplier=-1))
            link(pool.affine_select(out=mask_l[:, 1], in_=mask_l[:, 1], compare_op=ALU.is_ge, fill=NEG, base=0,
                                    pattern=[[-1, W]], channel_multiplier=1))
            link(pool.affine_select(out=mask_c[:], in_=mask_c[:], compare_op=ALU.is_ge, fill=NEG, base=CBS - 1,
                                    pattern=[[-P, T], [CBS, NB]], channel_multiplier=-1))
            link(pool.affine_select(out=block_m[:], in_=block_m[:], compare_op=ALU.is_ge, fill=0.0, base=0,
                                    pattern=[[-16, 2], [0, DH]], channel_multiplier=1))
            link(pool.affine_select(out=block_m[:], in_=block_m[:], compare_op=ALU.is_ge, fill=0.0, base=15,
                                    pattern=[[16, 2], [0, DH]], channel_multiplier=-1))
            for s in range(2):
                link(pool.memset(kz[s][0][64:128], 0.0))
                link(pool.memset(kz[s][1][0:64], 0.0))
            link(pool.memset(ck_bd[:], 0.0))
            link(pool.memset(cv_bd[:], 0.0))
            pool.memset(pc_T[:], 0.0).then_inc(consts, 1)
            pool.sem_inc(sim_read, FREE_SIM)
            pool.sem_inc(exp_done, FREE_EXP)
            pool.sem_inc(pt_done, FREE_PT)
            pool.sem_inc(pv_done, FREE_PV)
            pool.sem_inc(y_done, FREE_Y)
            for bank_free in (pt_evac, o_evac, y_added):
                pool.sem_inc(bank_free, FREE_BANK)
            pool.wait_ge(filled[1], pro("w23") // 2 + 1)
            pool.wait_ge(filled[0], pro("w22") // 2 + 1)
            pool.memset(kvb[:], 0.0).then_inc(zeroed, 1)
            pool.wait_ge(zeroed, 1)

            def build(q, slot, kv):
                for h in range(2):
                    r = slice(64 * h, 64 * h + 64)
                    src = (kz[slot][h] if kv == 0 else v_T)[r, 0:512].rearrange("p (n t) -> p t n", t=CBS)
                    pos = pos_T[r, bass.ds(q, 1), kv].rearrange("p a t -> p (a t)").unsqueeze(2).broadcast_to([64, CBS, NB // 2])
                    c = 32 * kv + 16 * h
                    pool.tensor_tensor(out=kvb[r, :, c:c + NB // 2], in0=src, in1=pos, op=ALU.add).then_inc(bd_ready, 1)
                    pool.wait_ge(bd_ready, q * 4 + (2 * kv + h + 1))

            pool.wait_ge(emptied[0], pro("v0") // 2 + 1)
            pool.wait_ge(emptied[1], pro("pos3") // 2 + 1)
            build(0, 0, 0)
            build(0, 0, 1)

            def pair(i, s, prep):
                pr = Pair(i, s)

                def scale(b):
                    lo = 0 if b else W
                    pool.wait_ge(r_ready, pr.p * T + (b + 1))
                    pool.tensor_tensor(out=prob[:, b % 4, :, lo:], in0=prob[:, b % 4, :, lo:],
                                       in1=rloc[:, b].unsqueeze(2).broadcast_to([P, 2, 2 * W - lo]), op=ALU.mult).then_inc(p_ready, 1)

                if prep:
                    pool.wait_ge(conv_done, pr.p + 1)
                    pool.wait_ge(emptied[0], pr.ordinal("k0"))
                    build(pr.p + 1, pr.nxt, 0)
                scale(0)
                if prep:
                    pool.wait_ge(emptied[0], pr.ordinal("v0"))
                    build(pr.p + 1, pr.nxt, 1)
                for b in range(1, T):
                    scale(b)

            with pool.Fori(0, NP // 2 - 1) as i:
                pair(i, 0, True)
                pair(i, 1, True)
            pair(NP // 2 - 1, 0, True)
            pair(NP // 2 - 1, 1, False)

        @block.tensor
        def _(pe):
            cnt = [0]

            def item_pro(name, fn):
                k = pro(name)
                if k >= 2:
                    pe.wait_ge(emptied[k % 2], k // 2)
                fn(ring[k % 2]).then_inc(filled[k % 2], 1)

            def tr4(blocks, idn=None):
                def f(ps):
                    for j, a in enumerate(blocks):
                        w = a.shape[0]
                        last = pe.transpose(ps[:, j * w:(j + 1) * w], a, ident[0:w, 0:w])
                    return last
                return f

            def project(slot, j, half):
                def f(ps):
                    for kt in range(KT):
                        last = pe.matmul(ps[:], proj_w[slot][:, kt, j, :], xr_T[:, kt, half * 512:half * 512 + 512],
                                         start=(kt == 0), stop=(kt == KT - 1))
                    return last
                return f

            def v_back(half):
                return tr4([v_T[:, (4 * half + j) * P:(4 * half + j + 1) * P] for j in range(4)])

            def conv(slot, t0, t1):
                for t in range(t0, t1):
                    g = 64 * (t % 2)
                    last = pe.matmul(p_conv[g:g + 64, 0:128], kvb[:, t, :],
                                     conv_w[slot][:, :, :, t].rearrange("p a o -> p (a o)"),
                                     start=(t < 2), stop=(t >= CBS - 2), skip_group_check=True)
                return last

            pe.wait_ge(consts, 2)
            pe.wait_ge(ln, 1)
            xr_v = xsq
            for kt in range(KT):
                for half in range(2):
                    item_pro(f"xr{2 * kt + half}", tr4([xr_v[:, 4 * half + j, kt * P:kt * P + P] for j in range(4)]))
            for kt in range(KT):
                for half in range(2):
                    item_pro(f"xn{2 * kt + half}", tr4([xc[:, 4 * half + j, kt * P:kt * P + P] for j in range(4)]))
            pe.wait_ge(pos_in, 32)
            for m in range(4):
                item_pro(f"pos{m}", tr4([pos_raw[:, 8 * m + 2 * j:8 * m + 2 * j + 2, :].rearrange("p h d -> p (h d)") for j in range(4)]))
            pe.wait_ge(wsum, 1)
            pe.matmul(p_y[:, 0:2], ones[:], wstat[:, 0:2], start=True, stop=True).then_inc(wtot, 1)
            pe.wait_ge(wq_ready, 1)
            for kt in range(KT):
                for half in range(2):
                    item_pro(f"w1{2 * kt + half}", tr4([w1_s[:, 4 * half + j, kt * P:kt * P + P] for j in range(4)]))
            for m in range(4):
                item_pro(f"w2{m}", tr4([w2_s[:, e, (2 * m + f) * P:(2 * m + f + 1) * P] for f in range(2) for e in range(2)]))
            pe.wait_ge(small_in, 80)
            for b in range(2):
                pe.wait_ge(emptied[b], pro(f"xr{2 + b}") // 2 + 1)
            for g in range(2):
                def f(ps, g=g):
                    for j in range(4):
                        for kt in range(KT):
                            last = pe.matmul(ps[:, j * 96:(j + 1) * 96], xr_T[:, kt, (4 * g + j) * P:(4 * g + j + 1) * P],
                                             wcomb[:, kt], start=(kt == 0), stop=(kt == KT - 1))
                    return last
                item_pro(f"g{g}", f)
            pe.wait_ge(proj_in[0], 32)
            for half in range(2):
                item_pro(f"k{half}", project(0, 1, half))
            for half in range(2):
                item_pro(f"v{half}", project(0, 2, half))
            for half in range(2):
                item_pro(f"q{half}", project(0, 0, half))
            for half in range(2):
                pe.wait_ge(emptied[half], pro(f"v{half}") // 2 + 1)
                item_pro(f"t{half}", v_back(half))
            for g in range(2):
                for b in range(2):
                    pe.wait_ge(emptied[b], pro(f"w2{2 + b}") // 2 + 1)
                for ft in range(FT):
                    def f(ps, g=g, ft=ft):
                        for kt in range(KT):
                            last = pe.matmul(ps[:], w1_T[:, kt, ft * P:(ft + 1) * P], xn_T[:, kt, g * 512:g * 512 + 512],
                                             start=(kt == 0), stop=(kt == KT - 1))
                        return last
                    item_pro(f"h{g}_{ft}", f)
                for b in range(2):
                    pe.wait_ge(emptied[b], pro(f"h{g}_{FT - 2 + b}") // 2 + 1)
                for j in range(2):
                    def f(ps, j=j):
                        for m in range(2):
                            for ft in range(FT):
                                last = pe.matmul(ps[:, m * DIM:(m + 1) * DIM], h_T[:, ft, (2 * j + m) * P:(2 * j + m + 1) * P],
                                                 w2_T[:, ft], start=(ft == 0), stop=(ft == FT - 1))
                        return last
                    item_pro(f"f{g}_{j}", f)
            pe.wait_ge(bd_ready, 4)
            pe.wait_ge(bd2_ready, 4)
            pe.wait_ge(conv_in[0], 64)
            conv(0, 0, CBS).then_inc(conv_done, 1)

            def pair(i, s, prep):
                pr = Pair(i, s)
                p, nx = pr.p, pr.nxt

                def item(name, fn):
                    b = int(name[1])
                    ring_wait_free(pe, b, pr.ordinal(name) if prep else pr.ordinal_last(name))
                    fn(ring[b]).then_inc(filled[b], 1)

                def sim(b):
                    if b == 1:
                        pe.wait_ge(y_added, p * 4 + FREE_BANK)
                    pe.wait_ge(sim_read, p * T + (b + 1))
                    lo = (b - 1) * W if b else 0
                    for h in range(2):
                        last = pe.matmul(p_sim[b % 2][:, h * 256 + (0 if b else W):(h + 1) * 256], q_T[s][:, b * P:(b + 1) * P],
                                         kz[s][h][:, lo:(b + 1) * W], start=True, stop=True)
                    last.then_inc(sim_done, 1)

                def turn_probs(b):
                    pe.wait_ge(p_ready, p * T + (b + 1))
                    pe.wait_ge(pt_evac, p * T + (b + FREE_BANK))
                    for h in range(2):
                        for c in range(0 if b else 1, 2):
                            last = pe.transpose(p_pt[:, (2 * h + c) * P:(2 * h + c + 1) * P],
                                                prob[:, b % 4, h, c * W:(c + 1) * W], ident[:])
                    last.then_inc(pt_done, 1)

                def pv(b):
                    pe.wait_ge(pt_evac, p * T + (b + 1 + FREE_BANK))
                    for c in range(0 if b else 1, 2):
                        for h in range(2):
                            last = pe.matmul(p_o[64 * h:64 * h + 64, (b % 4) * P:(b % 4 + 1) * P],
                                             v_tok[s][:, b - 1 + c, 64 * h:64 * h + 64], prob_T[:, b % 2, 2 * h + c, :],
                                             start=False, stop=True, skip_group_check=True)
                    last.then_inc(pv_done, 1)

                def comp_out(half):
                    pe.wait_ge(o_evac, p * 2 + (half + FREE_BANK))
                    pe.matmul(p_o[:], cv_bd[:], pc_T[:, half * 512:half * 512 + 512], start=True, stop=False,
                              skip_group_check=True)

                def y(j):
                    half = j // 2
                    if j % 2 == 0:
                        pe.wait_ge(o_evac, p * 2 + (half + 1 + FREE_BANK))
                        pe.wait_ge(outw_in[s], (i + 1) * 16)
                    bank_y = p_y
                    if j < 3:
                        pe.wait_ge(y_added, p * 4 + (j + FREE_BANK))
                    else:
                        pe.wait_ge(sim_read, p * T + (T + FREE_SIM))
                        bank_y = p_sim[1]
                    for m in range(2):
                        c = (2 * (j % 2) + m) * P
                        last = pe.matmul(bank_y[:, m * DIM:(m + 1) * DIM], o_T[:, half, c:c + P], out_w[s][:], start=True, stop=True)
                    last.then_inc(y_done, 1)

                pe.wait_ge(conv_evac, p + 1)
                for h in range(2):
                    pe.matmul(ck_ps[64 * h:64 * h + 64, 16 * h:16 * h + 16], conv_s[:, 0:64], sel[:, 16 * h:16 * h + 16],
                              start=True, stop=True, skip_group_check=True)
                pe.matmul(cv_ps, sel[:, 32:64], conv_s[:, 64:128], start=True, stop=True,
                          skip_group_check=True).then_inc(sel_done, 1)
                sim(0)
                if prep:
                    pe.wait_ge(proj_in[nx], (pr.nxt_use + 1) * 32)
                    item("k0", project(nx, 1, 0))
                    item("k1", project(nx, 1, 1))
                pe.wait_ge(ckcv, p + 1)
                for b in range(T):
                    last = pe.matmul(csim_ps[:, b].rearrange("p h n -> p (h n)"), q_T[s][:, b * P:(b + 1) * P], ck_bd[:],
                                     start=True, stop=True, skip_group_check=True)
                last.then_inc(csim_done, 1)
                sim(1)
                if prep:
                    item("v0", project(nx, 2, 0))
                    item("v1", project(nx, 2, 1))
                if prep:
                    item("q0", project(nx, 0, 0))
                    item("q1", project(nx, 0, 1))
                pe.wait_ge(pc_ready, p + 1)
                for half in range(2):
                    def f(ps, half=half):
                        for j in range(4):
                            last = pe.transpose(ps[0:32, j * P:(j + 1) * P],
                                                c_p[:, 4 * half + j].rearrange("p h n -> p (h n)"), ident[:])
                        return last
                    item(f"c{half}", f)
                for half in range(2):
                    pe.wait_ge(emptied[half], pr.ordinal(f"c{half}") if prep else pr.ordinal_last(f"c{half}"))
                comp_out(0)
                for b in range(T):
                    turn_probs(b)
                    if b + 2 < T:
                        sim(b + 2)
                    if prep:
                        if b == 0:
                            for half in range(2):
                                pe.wait_ge(emptied[half], pr.ordinal(f"v{half}"))
                                item(f"t{half}", v_back(half))
                        else:
                            if b == 1:
                                pe.wait_ge(bd_ready, p * 4 + 8)
                                pe.wait_ge(bd2_ready, p * 4 + 8)
                                pe.wait_ge(conv_in[nx], (pr.nxt_use + 1) * 64)
                                pe.wait_ge(csim_read, p + 1)
                            conv(nx, 8 * (b - 1), 8 * b)
                    if b == 4:
                        comp_out(1)
                    pv(b)
                    if b in (5, 6):
                        y(b - 5)
                if prep:
                    conv(nx, 56, CBS).then_inc(conv_done, 1)
                y(2)
                y(3)

            with pe.Fori(0, NP // 2 - 1) as i:
                pair(i, 0, True)
                pair(i, 1, True)
            pair(NP // 2 - 1, 0, True)
            pair(NP // 2 - 1, 1, False)

        @block.scalar
        def _(act):
            def item_pro(name):
                k = pro(name)
                assert k % 2 == 0
                act.wait_ge(filled[0], k // 2 + 1)
                return ring[0]

            for r in range(2):
                act.wait_ge(rt_in, r + 1)
                act.activation(stat[:, 4 + r], stat[:, 2 + r], ACT.Sqrt).then_inc(rt_out, 1)
            for kt in range(KT):
                ps = item_pro(f"xr{2 * kt}")
                act.wait_ge(small_in, 80)
                act.activation(xr_T[:, kt, 0:512], ps[:], ACT.Copy, scale=rms_c[:, kt:kt + 1]).then_inc(emptied[0], 1)
            for kt in range(KT):
                act.copy(xn_T[:, kt, 0:512], item_pro(f"xn{2 * kt}")[:]).then_inc(emptied[0], 1)
            for m in (0, 2):
                ps = item_pro(f"pos{m}")
                act.copy(pos_T[:, 4 * m:4 * m + 4].rearrange("p a b c -> p (a b c)"), ps[:]).then_inc(emptied[0], 1)
            for kt in range(KT):
                act.copy(w1_T[:, kt, 0:512], item_pro(f"w1{2 * kt}")[:]).then_inc(emptied[0], 1)
            for m in (0, 2):
                act.copy(w2_T[:, 2 * m:2 * m + 2].rearrange("p f e -> p (f e)"), item_pro(f"w2{m}")[:]).then_inc(emptied[0], 1)
            ps = item_pro("g0")
            act.copy(sig[:, 0:4].rearrange("p b n -> p (b n)"), ps[:, 0:384]).then_inc(emptied[0], 1)
            act.wait_ge(glog, 1)
            act.activation(sig[:], sig[:], ACT.Exp, scale=-1.0).then_inc(gexp, 1)

            def take(name, slot, ps, ins_wait=None):
                if name == "k0":
                    act.copy(kz[slot][0][0:64, 0:512], ps[0:64, :])
                    return act.copy(kz[slot][1][64:128, 0:512], ps[64:128, :])
                if name == "v0":
                    return act.copy(v_T[:, 0:512], ps[:])
                if name == "q0":
                    return act.mul(q_T[slot][:, 0:512], ps[:], SCALE)
                if name == "t0":
                    return act.copy(v_tok[slot][:, 0:4].rearrange("p b n -> p (b n)"), ps[:])
                return act.copy(pc_T[0:32, 0:512], ps[0:32, :])

            act.wait_ge(consts, 2)
            for name in ("k0", "v0", "q0", "t0"):
                take(name, 0, item_pro(name)).then_inc(emptied[0], 1)
            for g in range(2):
                for ft in range(0, FT, 2):
                    ps = item_pro(f"h{g}_{ft}")
                    act.activation(h_T[:, ft], ps[:], ACT.Gelu, bias=b1_c[:, ft:ft + 1]).then_inc(emptied[0], 1)
                    act.wait_ge(filled[1], pro(f"h{g}_{ft + 1}") // 2 + 1)
                    act.activation(h_T[:, ft + 1], ring[1][:], ACT.Gelu, bias=b1_c[:, ft + 1:ft + 2]).then_inc(emptied[1], 1)

            def pair(i, s, prep):
                pr = Pair(i, s)
                p = pr.p

                def evac(name):
                    act.wait_ge(filled[0], pr.ordinal(name) if prep else pr.ordinal_last(name))
                    take(name, s if name == "c0" else pr.nxt, ring[0]).then_inc(emptied[0], 1)

                def exps(b):
                    lo = 0 if b else W
                    act.wait_ge(sim_read, p * T + (b + 1 + FREE_SIM))
                    act.wait_ge(pt_done, p * T + (b + 1))
                    for h in range(2):
                        act.activation(prob[:, b % 4, h, lo:], s_neg[:, b % 2, h, lo:], ACT.Exp, bias=ncol[:, b, h:h + 1],
                                       scale=-1.0, accum_out=lsum[:, b, h:h + 1]).then_inc(exp_done, 1)

                exps(0)
                if prep:
                    evac("k0")
                act.wait_ge(cs_ready, p + 1)
                act.activation(c_e[:], c_s[:], ACT.Exp).then_inc(ce_ready, 1)
                exps(1)
                if prep:
                    evac("v0")
                if prep:
                    evac("q0")
                evac("c0")
                for b in range(T):
                    act.wait_ge(pt_done, p * T + (b + 1 + FREE_PT))
                    act.wait_ge(pv_done, p * T + (b - 1 + FREE_PV))
                    turned = p_pt[:].rearrange("p (a n) -> p a n", a=4)
                    which = slice(0, 4) if b else slice(1, 4, 2)
                    act.copy(prob_T[:, b % 2, which], turned[:, which]).then_inc(pt_evac, 1)
                    if b == 0 and prep:
                        evac("t0")
                    if b + 2 < T:
                        exps(b + 2)

            with act.Fori(0, NP // 2 - 1) as i:
                pair(i, 0, True)
                pair(i, 1, True)
            pair(NP // 2 - 1, 0, True)
            pair(NP // 2 - 1, 1, False)

        @block.vector
        def _(dve):
            n = [0]

            def link(ins):
                n[0] += 1
                ins.then_inc(dch, 1)
                dve.wait_ge(dch, n[0])

            def item_pro(name):
                k = pro(name)
                dve.wait_ge(filled[k % 2], k // 2 + 1)
                return ring[k % 2]

            def over(a):
                return a.unsqueeze(2).broadcast_to([P, T, DIM])

            dve.wait_ge(x_in, 16)
            link(dve.tensor_reduce(stat[:, 0], acc[:], AX.X, ALU.add))
            link(dve.tensor_scalar(stat[:, 1], stat[:, 0], 1.0 / DIM, None, ALU.mult))
            link(dve.tensor_tensor(out=xc[:], in0=acc[:], in1=over(stat[:, 1]), op=ALU.subtract))
            link(dve.tensor_tensor(out=xsq, in0=xc[:], in1=xc[:], op=ALU.mult))
            link(dve.tensor_reduce(stat[:, 0], xsq, AX.X, ALU.add))
            dve.tensor_scalar(stat[:, 2], stat[:, 0], 1.0 / DIM, LN_EPS, ALU.mult, ALU.add).then_inc(rt_in, 1)
            dve.wait_ge(rt_out, 1)
            link(dve.reciprocal(stat[:, 6], stat[:, 4]))
            link(dve.tensor_tensor(out=xc[:], in0=xc[:], in1=over(stat[:, 6]), op=ALU.mult))
            link(dve.tensor_tensor(out=xsq, in0=xc[:], in1=xc[:], op=ALU.mult))
            link(dve.tensor_reduce(stat[:, 0], xsq, AX.X, ALU.add))
            dve.tensor_scalar(stat[:, 3], stat[:, 0], 1.0 / DIM, RMS_EPS, ALU.mult, ALU.add).then_inc(rt_in, 1)
            dve.wait_ge(rt_out, 2)
            link(dve.reciprocal(stat[:, 7], stat[:, 5]))
            dve.tensor_tensor(out=xsq, in0=xc[:], in1=over(stat[:, 7]), op=ALU.mult).then_inc(ln, 1)

            dve.wait_ge(w12_in, 32)
            dve.tensor_reduce(wstat[:, 0:1], w1_s, AX.XY, ALU.add, apply_absolute_value=True)
            dve.tensor_reduce(wstat[:, 1:2], w2_s, AX.XY, ALU.add, apply_absolute_value=True).then_inc(wsum, 1)

            def evac_pro(name, dst, kt=None):
                ps = item_pro(name)
                if kt is None:
                    dve.tensor_copy(dst, ps[:]).then_inc(emptied[1], 1)
                else:
                    dve.tensor_scalar(dst, ps[:], rms_c[:, kt:kt + 1], None, ALU.mult).then_inc(emptied[1], 1)

            dve.wait_ge(small_in, 80)
            for kt in range(KT):
                evac_pro(f"xr{2 * kt + 1}", xr_T[:, kt, 512:1024], kt)
            for kt in range(KT):
                evac_pro(f"xn{2 * kt + 1}", xn_T[:, kt, 512:1024])
            for m in (1, 3):
                evac_pro(f"pos{m}", pos_T[:, 4 * m:4 * m + 4].rearrange("p a b c -> p (a b c)"))
            dve.wait_ge(wtot, 1)
            link(dve.tensor_scalar(wstat[:, 2:4], p_y[:, 0:2], 1.0 / (DFF * DIM), Q_EPS, ALU.mult, ALU.max))
            link(dve.reciprocal(wstat[:, 4:6], wstat[:, 2:4]))
            for j, w_s in enumerate((w1_s, w2_s)):
                link(dve.tensor_scalar(w_s, w_s, wstat[:, 4 + j:5 + j], 1.0, ALU.mult, ALU.min))
                link(dve.tensor_scalar(w_s, w_s, -1.0, ROUND, ALU.max, ALU.add))
                last = dve.tensor_scalar(w_s, w_s, -ROUND, None, ALU.add)
            last.then_inc(wq_ready, 1)
            for kt in range(KT):
                evac_pro(f"w1{2 * kt + 1}", w1_T[:, kt, 512:1024])
            for m in (1, 3):
                evac_pro(f"w2{m}", w2_T[:, 2 * m:2 * m + 2].rearrange("p f e -> p (f e)"))
            ps = item_pro("g1")
            dve.tensor_copy(sig[:, 4:8].rearrange("p b n -> p (b n)"), ps[:, 0:384]).then_inc(emptied[1], 1)
            for b in range(2):
                dve.wait_ge(emptied[b], pro(f"g{b}") // 2 + 1)
            dve.tensor_tensor(out=sig[:], in0=sig[:], in1=bc_r[:].unsqueeze(1).broadcast_to([P, T, 3 * H]), op=ALU.add).then_inc(glog, 1)
            dve.wait_ge(gexp, 1)
            link(dve.tensor_scalar(sig[:], sig[:], 1.0, None, ALU.add))
            link(dve.reciprocal(sig[:], sig[:]))
            sg = sig[:].rearrange("p b (q h k) -> p q b h k", h=2, k=3)
            for q in range(NP):
                dve.tensor_tensor(out=gate[:, q, 0], in0=sg[:, q, :, :, 0], in1=sg[:, q, :, :, 1], op=ALU.add)
                dve.tensor_copy(gate[:, q, 1], sg[:, q, :, :, 2]).then_inc(gates, 1)

            def take(name, slot, ps):
                if name == "k1":
                    dve.tensor_copy(kz[slot][0][0:64, 512:1024], ps[0:64, :])
                    return dve.tensor_copy(kz[slot][1][64:128, 512:1024], ps[64:128, :])
                if name == "v1":
                    return dve.tensor_copy(v_T[:, 512:1024], ps[:])
                if name == "q1":
                    return dve.tensor_scalar(q_T[slot][:, 512:1024], ps[:], SCALE, None, ALU.mult)
                if name == "t1":
                    return dve.tensor_copy(v_tok[slot][:, 4:8].rearrange("p b n -> p (b n)"), ps[:])
                return dve.tensor_copy(pc_T[0:32, 512:1024], ps[0:32, :])

            def build(q, kv, ps):
                for h in range(2):
                    r = slice(64 * h, 64 * h + 64)
                    pos = pos_T[r, bass.ds(q, 1), kv].rearrange("p a t -> p (a t)").unsqueeze(2).broadcast_to([64, CBS, NB // 2])
                    c = 32 * kv + 16 * h + NB // 2
                    dve.tensor_tensor(out=kvb[r, :, c:c + NB // 2], in0=ps[r, :].rearrange("p (n t) -> p t n", t=CBS),
                                      in1=pos, op=ALU.add).then_inc(bd2_ready, 1)

            dve.wait_ge(consts, 2)
            dve.wait_ge(zeroed, 1)
            dve.wait_ge(emptied[0], pro("pos2") // 2 + 1)
            for name in ("k1", "v1", "q1", "t1"):
                ps = item_pro(name)
                if name in ("k1", "v1"):
                    build(0, int(name == "v1"), ps)
                take(name, 0, ps).then_inc(emptied[1], 1)
            b2b = b2_r[:].unsqueeze(1).broadcast_to([P, 2, DIM])
            for m in range(4):
                link(dve.tensor_tensor(out=acc[:, 2 * m:2 * m + 2], in0=acc[:, 2 * m:2 * m + 2], in1=b2b, op=ALU.add))
            for g in range(2):
                for j in range(2):
                    ps = item_pro(f"f{g}_{j}")
                    a = acc[:, 4 * g + 2 * j:4 * g + 2 * j + 2].rearrange("p b c -> p (b c)")
                    dve.tensor_tensor(out=a, in0=a, in1=ps[:], op=ALU.add).then_inc(emptied[pro(f"f{g}_{j}") % 2], 1)

            def conv_out(q, slot, use):
                dve.wait_ge(conv_done, q + 1)
                dve.wait_ge(bias_in[slot], (use + 1) * 64)
                dve.tensor_tensor(out=conv_s[:], in0=p_conv[:, 0:128], in1=conv_b[slot][:], op=ALU.add).then_inc(conv_evac, 1)

            conv_out(0, 0, 0)
            dve.wait_ge(gates, NP)

            CCHAIN, LCHAIN = 5, 8

            def pair(i, s, prep):
                pr = Pair(i, s)
                p = pr.p
                c, l = [0], [0]

                def link_c(ins):
                    c[0] += 1
                    ins.then_inc(cchain, 1)
                    dve.wait_ge(cchain, p * CCHAIN + c[0])

                def evac(name):
                    dve.wait_ge(filled[1], pr.ordinal(name) if prep else pr.ordinal_last(name))
                    if name in ("k1", "v1"):
                        build(p + 1, int(name == "v1"), ring[1])
                    take(name, s if name == "c1" else pr.nxt, ring[1]).then_inc(emptied[1], 1)

                def scores(b):
                    c0 = 0 if b else 1
                    dve.wait_ge(sim_done, p * T + (b + 1))
                    dve.wait_ge(exp_done, (p * T + b) * 2 + 2)
                    dve.sem_inc(step_begun, 1)
                    for h in range(2):
                        ins = dve.tensor_tensor_reduce(
                            out=s_neg[:, b % 2, h, c0 * W:].rearrange("p (c j) -> p c j", j=W),
                            in0=p_sim[b % 2][:, h * 256 + c0 * W:(h + 1) * 256].rearrange("p (c j) -> p c j", j=W),
                            in1=mask_l[:, c0:], scale=-1.0, scalar=-NEG * 2, op0=ALU.add, op1=ALU.min,
                            accum_out=ncol[:, b, h:h + 1])
                    ins.then_inc(sim_read, 1)

                def row_scale(b):
                    l[0] += 1
                    dve.wait_ge(exp_done, (p * T + b) * 2 + (2 + FREE_EXP))
                    dve.reciprocal(rinv[:, b], lsum[:, b]).then_inc(lchain, 1)
                    dve.wait_ge(lchain, p * LCHAIN + l[0])
                    dve.tensor_tensor(out=rloc[:, b], in0=rinv[:, b], in1=gate_p[:, 0, b], op=ALU.mult).then_inc(r_ready, 1)

                def y_add(j):
                    dve.wait_ge(y_done, p * 4 + (j + 1 + FREE_Y))
                    dve.wait_ge(y_added, p * 4 + (j + FREE_BANK))
                    a = acc[:, 2 * j:2 * j + 2].rearrange("p b c -> p (b c)")
                    dve.tensor_tensor(out=a, in0=a, in1=(p_y if j < 3 else p_sim[1])[:], op=ALU.add).then_inc(y_added, 1)

                def o_out(half):
                    dve.wait_ge(pv_done, p * T + (4 * half + 4 + FREE_PV))
                    dve.wait_ge(y_done, p * 4 + (2 * half - 2 + FREE_Y))
                    dve.tensor_copy(o_T[:, half], p_o[:]).then_inc(o_evac, 1)

                dve.wait_ge(sel_done, p + 1)
                for h in range(2):
                    dve.tensor_copy(ck_bd[64 * h:64 * h + 64, 16 * h:16 * h + 16], ck_ps[64 * h:64 * h + 64, 16 * h:16 * h + 16])
                dve.tensor_tensor(out=cv_bd[0:32].rearrange("p (h o) -> p h o", h=2), in0=cv_ps.unsqueeze(1).broadcast_to([32, 2, DH]),
                                  in1=block_m[:], op=ALU.mult).then_inc(ckcv, 1)
                link_c(dve.tensor_copy(gate_p[:].rearrange("p a b c -> p (a b c)"), gate[:, bass.ds(p, 1)].rearrange("p q a b c -> p (q a b c)")))
                scores(0)
                if prep:
                    evac("k1")
                dve.wait_ge(csim_done, p + 1)
                dve.tensor_tensor(out=c_s[:], in0=csim_ps, in1=mask_c[:].unsqueeze(2).broadcast_to([P, T, 2, NB]), op=ALU.add).then_inc(csim_read, 1)
                dve.wait_ge(csim_read, p + 1)
                cs2 = c_s[:].rearrange("p b h n -> p (b h) n")
                link_c(dve.tensor_reduce(c_m[:], cs2, AX.X, ALU.max))
                dve.tensor_tensor(out=cs2, in0=cs2, in1=c_m[:].unsqueeze(2).broadcast_to([P, 2 * T, NB]), op=ALU.subtract).then_inc(cs_ready, 1)
                scores(1)
                if prep:
                    evac("v1")
                dve.wait_ge(ce_ready, p + 1)
                ce2 = c_e[:].rearrange("p b h n -> p (b h) n")
                link_c(dve.tensor_reduce(c_l[:], ce2, AX.X, ALU.add))
                link_c(dve.reciprocal(c_r[:], c_l[:]))
                link_c(dve.tensor_tensor(out=c_g[:], in0=c_r[:], in1=gate_p[:, 1].rearrange("p b h -> p (b h)"), op=ALU.mult))
                dve.tensor_tensor(out=c_p[:].rearrange("p b h n -> p (b h) n"), in0=ce2,
                                  in1=c_g[:].unsqueeze(2).broadcast_to([P, 2 * T, NB]), op=ALU.mult).then_inc(pc_ready, 1)
                row_scale(0)
                row_scale(1)
                if prep:
                    evac("q1")
                evac("c1")
                for b in range(T):
                    if b == 0 and prep:
                        evac("t1")
                    if b == 4:
                        o_out(0)
                    if b + 2 < T:
                        scores(b + 2)
                        row_scale(b + 2)
                    if b in (6, 7):
                        y_add(b - 6)
                o_out(1)
                if prep:
                    conv_out(p + 1, pr.nxt, pr.nxt_use)
                y_add(2)
                y_add(3)
                assert c[0] == CCHAIN and l[0] == LCHAIN, (c, l)

            with dve.Fori(0, NP // 2 - 1) as i:
                pair(i, 0, True)
                pair(i, 1, True)
            pair(NP // 2 - 1, 0, True)
            pair(NP // 2 - 1, 1, False)


_INS = ["L0_attn_inp", "L0_attn_rms_w", "L0_attn_w_qkv", "L0_attn_k_pos", "L0_attn_v_pos", "L0_attn_kc_w",
        "L0_attn_kc_b", "L0_attn_vc_w", "L0_attn_vc_b", "L0_attn_w_comb", "L0_attn_b_comb", "L0_attn_w_out",
        "L0_ffn_w1", "L0_ffn_b1", "L0_ffn_w2", "L0_ffn_b2"]


def kernel(**inputs):
    import numpy as _np
    import concourse.bacc as _bacc
    from concourse import mybir as _mybir
    from concourse.bass_utils import run_bass_kernel_spmd as _run

    nc = _bacc.Bacc("TRN2", target_bir_lowering=False, num_devices=1)
    arrays, args = {}, []
    for name in _INS:
        a = _np.ascontiguousarray(inputs[name])
        arrays[f"in_{name}_dram"] = a
        args.append(nc.dram_tensor(f"in_{name}_dram", a.shape, _mybir.dt.from_np(a.dtype), kind="ExternalInput").ap())
    args.append(nc.dram_tensor("out_0_dram", (1, S, DIM), F32, kind="ExternalOutput").ap())
    layer(nc, *args)
    r = _run(nc, [arrays], core_ids=[0])
    return r.results[0]["out_0_dram"]
```

```python
from contextlib import ExitStack

import concourse.bass as bass
from concourse import mybir

F32 = mybir.dt.float32
F32R = mybir.dt.float32r
ALU = mybir.AluOpType
ACT = mybir.ActivationFunctionType
AX = mybir.AxisListType

P = 128
S, DIM, H, DH = 1024, 256, 32, 64
W = 128
CBS = 64
NB = S // CBS
T = S // P
KT = DIM // P
NP = H // 2
DFF = 1024
FT = DFF // P
SCALE = DH ** -0.5
NEG = -1e30
LN_EPS, RMS_EPS, Q_EPS = 1e-5, 1.1920929e-07, 1e-8
ROUND = 1.5 * 2 ** 23

PRO_ITEMS = ([f"{n}{j}" for n in ("xr", "pos") for j in range(4)] + ["k0", "k1", "v0", "v1"]
             + [f"xn{j}" for j in range(4)] + ["q0", "q1", "t0", "t1", "g0", "g1"]
             + [f"{n}{j}" for n in ("w1", "w2") for j in range(4)])
FFN_ITEMS = [f"h{g}_{f}" for g in range(2) for f in range(FT)]
FFN_OUT = [f"f{g}_{j}" for g in range(2) for j in range(2)]
ORDER = PRO_ITEMS + [x for g in range(2) for x in FFN_ITEMS[g * FT:(g + 1) * FT] + FFN_OUT[g * 2:g * 2 + 2]]
RING0 = len(ORDER)
PAIR_ITEMS = ["k0", "k1", "v0", "v1", "q0", "q1", "c0", "c1", "t0", "t1"]
RING_PER_PAIR = len(PAIR_ITEMS)
assert RING0 % 2 == 0 and all(int(x[-1]) % 2 == n % 2 for n, x in enumerate(ORDER))


def layer(nc, inp, rms_w, w_qkv, k_pos, v_pos, kc_w, kc_b, vc_w, vc_b, w_comb, b_comb, w_out,
          w1, b1, w2, b2, out):
    with ExitStack() as ctx:
        def sb(name, shape, dtype=F32, at=ctx):
            return at.enter_context(nc.sbuf_tensor(name, shape, dtype))

        def sem(name):
            return ctx.enter_context(nc.semaphore(name))

        acc = sb("acc", [P, T, DIM])
        xr_h = sb("xr_h", [P, KT, S], F32R)
        xr_l = sb("xr_l", [P, KT, S], F32R)
        pw_h = sb("pw_h", [P, KT, 3, P], F32R)
        pw_l = sb("pw_l", [P, KT, 3, P], F32R)
        pos_T = sb("pos_T", [P, NP, 2, CBS])
        with ExitStack() as early:
            raw = sb("raw", [P, 8192], at=early)
        with ExitStack() as early:
            g_h = sb("g_h", [P, FT, 512], F32R, at=early)
            g_l = sb("g_l", [P, FT, 512], F32R, at=early)
        conv_w = [sb(f"conv_w{s}", [P, 2, DH, CBS]) for s in (1, 0)][::-1]
        proj_w = [sb(f"proj_w{s}", [P, KT, 3, P]) for s in range(2)]
        out_w = [sb(f"out_w{s}", [P, DIM]) for s in range(2)]
        conv_b = [sb(f"conv_b{s}", [P, P]) for s in range(2)]
        with ExitStack() as early:
            xn_h = sb("xn_h", [P, KT, S], F32R, at=early)
            xn_l = sb("xn_l", [P, KT, S], F32R, at=early)
        kqv1 = sb("kqv1", [P, 4, S])
        kz = [[sb(f"kz{s}{h}", [P, S]) for h in range(2)] for s in range(1)]
        kz.append([kqv1[:, 0], kqv1[:, 1]])
        q_T = [sb("q_T0", [P, S]), kqv1[:, 2]]
        v_T = sb("v_T", [P, S])
        v_tok = [sb("v_tok0", [P, T, P]), kqv1[:, 3].rearrange("p (t n) -> p t n", t=T)]
        kvb = sb("kvb", [P, CBS, 64])
        s_neg = sb("s_neg", [P, 2, 2, 2 * W])
        with ExitStack() as early:
            xr_xn = sb("xr_xn", [P, T, DIM], at=early)
            xr_T = sb("xr_T", [P, KT, S], at=early)
        with ExitStack() as early:
            w1_T = sb("w1_T", [P, KT, DFF], F32R, at=early)
            w2_T = sb("w2_T", [P, FT, DIM], F32R, at=early)
        prob = sb("prob", [P, 4, 2, 2 * W])
        turned_o = sb("turned_o", [P, 2, 2, 4 * P])
        prob_T = turned_o[:, 0].rearrange("p a (c n) -> p a c n", c=4)
        o_T = turned_o[:, 1]
        ncol = sb("ncol", [P, T, 2])
        lsum = sb("lsum", [P, T, 2])
        rinv = sb("rinv", [P, T, 2])
        rloc = sb("rloc", [P, T, 2])
        gate_p = sb("gate_p", [P, 2, T, 2])
        gate = sb("gate", [P, NP, 2, T, 2])
        c_s = sb("c_s", [P, T, 2, NB])
        c_e = sb("c_e", [P, T, 2, NB])
        c_p = sb("c_p", [P, T, 2, NB])
        c_m = sb("c_m", [P, T * 2])
        c_l = sb("c_l", [P, T * 2])
        c_r = sb("c_r", [P, T * 2])
        c_g = sb("c_g", [P, T * 2])
        pc_T = sb("pc_T", [P, S])
        conv_s = sb("conv_s", [P, P])
        ck_bd = sb("ck_bd", [P, 2 * NB])
        cv_bd = sb("cv_bd", [P, P])
        ident = sb("ident", [P, P])
        sel = sb("sel", [P, 64])
        ones = sb("ones", [P, P])
        mask_l = sb("mask_l", [P, 2, W])
        mask_c = sb("mask_c", [P, T, NB])
        block_m = sb("block_m", [32, 2, DH])
        rms_c = sb("rms_c", [P, KT])
        b1_c = sb("b1_c", [P, FT])
        b2_r = sb("b2_r", [P, DIM])
        bc_r = sb("bc_r", [P, 3 * H])
        wcomb = sb("wcomb", [P, KT, 3 * H])
        stat = sb("stat", [P, 8, T])
        wstat = sb("wstat", [P, 12])
        sig = sb("sig", [P, T, 3 * H])
        xr = xc = xr_xn
        w1_s = raw[:, 0:2048].rearrange("p (j c) -> p j c", j=FT)
        w2_s = raw[:, 2048:4096].rearrange("p (j f) -> p j f", j=2)
        pos_raw = raw[:, 4096:6144].rearrange("p (h d) -> p h d", h=H)
        w_abs = s_neg[:].rearrange("p a b c -> p (a b c)")
        g_f = s_neg[:].rearrange("p a b c -> p (a b c)").rearrange("p (a n) -> p a n", a=2)
        bn = sb("bn", [P, T, 6])
        mv = sb("mv", [P, T, 2])

        bank = [ctx.enter_context(nc.psum_tensor(f"bank{n}", [P, 512], F32)) for n in range(8)]
        ring, p_conv, p_sim, p_pt, p_o, p_y = bank[0:2], bank[2], bank[3:5], bank[5], bank[6], bank[7]
        ck_ps = p_conv[:, 128:160]
        cv_ps = p_conv[0:32, 192:256]
        csim_ps = p_conv[:, 256:512].rearrange("p (b h n) -> p b h n", b=T, h=2)

        x_in = [sem(f"x_in{g}") for g in range(4)]
        rms_in, small_in, w12_in, pos_in = sem("rms_in"), sem("small_in"), sem("w12_in"), sem("pos_in")
        proj_in = [sem(f"proj_in{s}") for s in range(2)]
        conv_in = [sem(f"conv_in{s}") for s in range(2)]
        bias_in = [sem(f"bias_in{s}") for s in range(2)]
        outw_in = [sem(f"outw_in{s}") for s in range(2)]
        consts = sem("consts")
        xr_ready, xn_ready = sem("xr_ready"), sem("xn_ready")
        rt_in, rt_out = sem("rt_in"), sem("rt_out")
        dch = sem("dch")
        pch = sem("pch")
        wabs, wsum, wtot, wq_ready = sem("wabs"), sem("wsum"), sem("wtot"), sem("wq_ready")
        wscale, w2q_ready, b2_added = sem("wscale"), sem("w2q_ready"), sem("b2_added")
        glog, gexp, gates = sem("glog"), sem("gexp"), sem("gates")
        filled = [sem(f"ring_filled{n}") for n in range(2)]
        emptied = [sem(f"ring_emptied{n}") for n in range(2)]
        bd2_ready, bd_ready, conv_done, conv_evac = sem("bd2_ready"), sem("bd_ready"), sem("conv_done"), sem("conv_evac")
        sel_done, ckcv, csim_done = sem("sel_done"), sem("ckcv"), sem("csim_done")
        csim_read, cs_ready, ce_ready, pc_ready = sem("csim_read"), sem("cs_ready"), sem("ce_ready"), sem("pc_ready")
        w_split = sem("w_split")
        xr_T_ready, x_split = sem("xr_T_ready"), sem("x_split")
        xn_h_ready, gh_ready, g_split = sem("xn_h_ready"), sem("gh_ready"), sem("g_split")
        cchain, lchain = sem("cchain"), sem("lchain")
        sim_done, sim_read, exp_done = sem("sim_done"), sem("sim_read"), sem("exp_done")
        r_ready, p_ready, pt_done, pt_evac = sem("r_ready"), sem("p_ready"), sem("pt_done"), sem("pt_evac")
        pv_done, o_evac, y_done, y_added = sem("pv_done"), sem("o_evac"), sem("y_done"), sem("y_added")
        step_begun, split_begun = sem("step_begun"), sem("split_begun")
        stored = sem("stored")

        FREE_SIM, FREE_EXP, FREE_PT, FREE_PV, FREE_Y, FREE_BANK = 2, 4, 4, 2, 3, 1

        def wait_filled(eng, k):
            eng.wait_ge(filled[k % 2], k // 2 + 1)

        def pro(name):
            return ORDER.index(name)

        class Pair:

            def __init__(self, i, s):
                self.i, self.s, self.p = i, s, i * 2 + s
                self.nxt = None if s == -1 else (1 - s)
                self.nxt_use = i + s

            def ordinal_last(self, name):
                return self.p * (RING_PER_PAIR // 2) + (RING0 // 2 + 1)

            def ordinal(self, name):
                return self.p * (RING_PER_PAIR // 2) + (RING0 // 2 + PAIR_ITEMS.index(name) // 2 + 1)

        def ring_wait_free(pe, b, ordinal):
            pe.wait_ge(emptied[b], ordinal - 1)

        block = ctx.enter_context(nc.Block())

        @block.sync
        def _(sp):
            def load_proj(q, s):
                for kt in range(KT):
                    sp.dma_start(proj_w[s][:, kt], w_qkv[kt * P:(kt + 1) * P].rearrange("c (j n) -> c j n", j=3)[:, :, bass.ds(q * P, P)]).then_inc(proj_in[s], 16)

            def load_conv(q, s):
                for kv, src in enumerate((kc_w, vc_w)):
                    for h in range(2):
                        sp.dma_start(conv_w[s][64 * h:64 * h + 64, kv],
                                     src[bass.ds(q * 2 + h, 1)].rearrange("a o i t -> (a i) o t")).then_inc(conv_in[s], 16)

            def load_bias(q, s):
                for kv, src in enumerate((kc_b, vc_b)):
                    for h in range(2):
                        r = 32 * kv + 16 * h
                        sp.dma_start(conv_b[s][r:r + 16, 64 * kv:64 * kv + 64],
                                     src[bass.ds(q * 2 + h, 1)].broadcast_to([16, DH])).then_inc(bias_in[s], 16)

            def load_outw(q, s):
                sp.dma_start(out_w[s][:], w_out[bass.ds(q * P, P)]).then_inc(outw_in[s], 16)

            for g in range(4):
                sp.dma_start(acc[:, 2 * g:2 * g + 2], inp[0, 256 * g:256 * g + 256].rearrange("(b p) c -> p b c", p=P)).then_inc(x_in[g], 16)
            sp.dma_start(rms_c[:], rms_w.rearrange("(k p) -> p k", p=P), allow_slow_non_contiguous=True).then_inc(rms_in, 16)
            load_proj(0, 0)
            for n, src in enumerate((k_pos, v_pos)):
                sp.dma_start(pos_raw[64 * n:64 * n + 64], src.rearrange("h t d -> t h d")).then_inc(pos_in, 16)
            sp.dma_start(w1_s, w1.rearrange("(j p) c -> p j c", p=P)).then_inc(w12_in, 16)
            sp.dma_start(w2_s, w2.rearrange("(j p) f -> p j f", p=P)).then_inc(w12_in, 16)
            sp.dma_start(b1_c[:], b1.rearrange("(f p) -> p f", p=P), allow_slow_non_contiguous=True).then_inc(small_in, 16)
            sp.dma_start(b2_r[:], b2.partition_broadcast(P)).then_inc(small_in, 16)
            sp.dma_start(bc_r[:], b_comb.partition_broadcast(P)).then_inc(small_in, 16)
            sp.dma_start(wcomb[:], w_comb.rearrange("(k p) n -> p k n", p=P)).then_inc(small_in, 16)
            load_conv(0, 0)
            sp.wait_ge(consts, 1)
            load_bias(0, 0)
            load_outw(0, 0)
            load_proj(1, 1)
            load_bias(1, 1)
            load_outw(1, 1)
            sp.wait_ge(filled[1], pro("f1_1") // 2 + 1)
            load_conv(1, 1)

            def pair(i, s):
                p = i * 2 + s
                sp.wait_ge(filled[1], p * (RING_PER_PAIR // 2) + (RING0 // 2 - 2))
                load_proj(p + 2, s)
                sp.wait_ge(conv_evac, p + 1)
                load_conv(p + 2, s)
                load_bias(p + 2, s)
                sp.wait_ge(y_done, p * 4 + (FREE_Y + 4))
                load_outw(p + 2, s)

            with sp.Fori(0, NP // 2 - 1) as i:
                pair(i, 0)
                pair(i, 1)
            for m in range(4):
                sp.wait_ge(y_added, 4 * (NP - 1) + m + 1 + FREE_BANK)
                sp.dma_start(out[0, 256 * m:256 * m + 256].rearrange("(b p) c -> p b c", p=P),
                             acc[:, 2 * m:2 * m + 2]).then_inc(stored, 16)
            sp.wait_ge(stored, 64)

        @block.gpsimd
        def _(pool):
            n = [0]

            def link(ins):
                n[0] += 1
                ins.then_inc(pch, 1)
                pool.wait_ge(pch, n[0])

            for s in range(2):
                link(pool.memset(conv_b[s][:], 0.0))
            pool.sem_inc(consts, 1)
            link(pool.memset(ident[:], 0.0))
            link(pool.affine_select(out=ident[:], in_=ident[:], compare_op=ALU.not_equal, fill=1.0, base=0,
                                    pattern=[[-1, P]], channel_multiplier=1))
            pool.sem_inc(consts, 1)
            link(pool.memset(ones[:], 1.0))

            def split_weights(slot, use, q):
                split_high(slot, use, 0)
                split_high(slot, use, 1)
                split_low(slot, q, 0)
                split_low(slot, q, 1)

            def split_high(slot, use, kt):
                if kt == 0:
                    pool.wait_ge(proj_in[slot], (use + 1) * 32)
                    pool.sem_inc(split_begun, 1)
                pool.tensor_copy(out=pw_h[:, kt], in_=proj_w[slot][:, kt]).then_inc(w_split, 1)

            def split_low(slot, q, kt):
                pool.wait_ge(w_split, q * 4 + (kt + 2))
                pool.tensor_tensor(out=pw_l[:, kt], in0=proj_w[slot][:, kt], in1=pw_h[:, kt], op=ALU.subtract).then_inc(w_split, 1)
                if kt == KT - 1:
                    pool.wait_ge(w_split, q * 4 + 4)

            split_weights(0, 0, 0)
            link(pool.memset(kz[0][0][64:128], 0.0))
            link(pool.memset(kz[0][1][0:64], 0.0))
            link(pool.memset(kvb[:], 0.0))
            pool.sem_inc(consts, 1)
            link(pool.memset(mask_l[:], 0.0))
            link(pool.memset(mask_c[:], 0.0))
            link(pool.memset(block_m[:], 1.0))
            link(pool.tensor_tensor(out=sel[:], in0=ident[:, 0:64], in1=ident[:, 64:128], op=ALU.add))
            link(pool.affine_select(out=mask_l[:, 0], in_=mask_l[:, 0], compare_op=ALU.is_ge, fill=NEG, base=0,
                                    pattern=[[1, W]], channel_multiplier=-1))
            link(pool.affine_select(out=mask_l[:, 1], in_=mask_l[:, 1], compare_op=ALU.is_ge, fill=NEG, base=0,
                                    pattern=[[-1, W]], channel_multiplier=1))
            link(pool.affine_select(out=mask_c[:], in_=mask_c[:], compare_op=ALU.is_ge, fill=NEG, base=CBS - 1,
                                    pattern=[[-P, T], [CBS, NB]], channel_multiplier=-1))
            link(pool.affine_select(out=block_m[:], in_=block_m[:], compare_op=ALU.is_ge, fill=0.0, base=0,
                                    pattern=[[-16, 2], [0, DH]], channel_multiplier=1))
            link(pool.affine_select(out=block_m[:], in_=block_m[:], compare_op=ALU.is_ge, fill=0.0, base=15,
                                    pattern=[[16, 2], [0, DH]], channel_multiplier=-1))
            link(pool.memset(ck_bd[:], 0.0))
            link(pool.memset(cv_bd[:], 0.0))
            pool.memset(pc_T[:], 0.0).then_inc(consts, 1)
            pool.sem_inc(sim_read, FREE_SIM)
            pool.sem_inc(exp_done, FREE_EXP)
            pool.sem_inc(pt_done, FREE_PT)
            pool.sem_inc(pv_done, FREE_PV)
            pool.sem_inc(y_done, FREE_Y)
            for bank_free in (pt_evac, o_evac, y_added):
                pool.sem_inc(bank_free, FREE_BANK)

            def build(q, slot, kv):
                for h in range(2):
                    r = slice(64 * h, 64 * h + 64)
                    src = (kz[slot][h] if kv == 0 else v_T)[r, 0:512].rearrange("p (n t) -> p t n", t=CBS)
                    pos = pos_T[r, bass.ds(q, 1), kv].rearrange("p a t -> p (a t)").unsqueeze(2).broadcast_to([64, CBS, NB // 2])
                    c = 32 * kv + 16 * h
                    pool.tensor_tensor(out=kvb[r, :, c:c + NB // 2], in0=src, in1=pos, op=ALU.add).then_inc(bd_ready, 1)
                    pool.wait_ge(bd_ready, q * 4 + (2 * kv + h + 1))

            pool.wait_ge(wscale, 1)
            pool.tensor_scalar(w2_s, w2_s, wstat[:, 9:10], 1.0, ALU.mult, ALU.min).then_inc(w2q_ready, 1)
            pool.wait_ge(w2q_ready, 1)
            pool.tensor_scalar(w2_s, w2_s, -1.0, ROUND, ALU.max, ALU.add).then_inc(w2q_ready, 1)
            pool.wait_ge(w2q_ready, 2)
            pool.wait_ge(small_in, 64)
            pool.wait_ge(xn_ready, T)
            b2b = b2_r[:].unsqueeze(1).broadcast_to([P, 2, DIM])
            for m in range(4):
                pool.tensor_tensor(out=acc[:, 2 * m:2 * m + 2], in0=acc[:, 2 * m:2 * m + 2], in1=b2b, op=ALU.add).then_inc(b2_added, 1)
            pool.wait_ge(b2_added, 4)
            pool.wait_ge(emptied[0], pro("v0") // 2 + 1)
            pool.wait_ge(emptied[1], pro("pos3") // 2 + 1)
            build(0, 0, 0)
            build(0, 0, 1)
            pool.wait_ge(filled[1], pro("q1") // 2 + 1)
            split_weights(1, 0, 1)
            for b in range(2):
                pool.wait_ge(filled[b], pro(f"h1_{FT - 2 + b}") // 2 + 1)
            link(pool.memset(kz[1][0][64:128], 0.0))
            link(pool.memset(kz[1][1][0:64], 0.0))
            pool.sem_inc(consts, 1)

            def pair(i, s, prep, split):
                pr = Pair(i, s)

                def scale(b):
                    lo = 0 if b else W
                    pool.wait_ge(r_ready, pr.p * T + (b + 1))
                    pool.tensor_tensor(out=prob[:, b % 4, :, lo:], in0=prob[:, b % 4, :, lo:],
                                       in1=rloc[:, b].unsqueeze(2).broadcast_to([P, 2, 2 * W - lo]), op=ALU.mult).then_inc(p_ready, 1)

                scale(0)
                if prep:
                    pool.wait_ge(conv_done, pr.p + 1)
                    pool.wait_ge(emptied[0], pr.ordinal("k0"))
                    build(pr.p + 1, pr.nxt, 0)
                    pool.wait_ge(emptied[0], pr.ordinal("v0"))
                    build(pr.p + 1, pr.nxt, 1)
                for b in range(1, T):
                    scale(b)
                    if split and b == 2:
                        pool.wait_ge(filled[1], pr.ordinal("q1"))
                    if split and b in (2, 3):
                        split_high(s, i + 1, b - 2)
                    if split and b in (4, 5):
                        split_low(s, pr.p + 2, b - 4)

            with pool.Fori(0, NP // 2 - 1) as i:
                pair(i, 0, True, True)
                pair(i, 1, True, True)
            pair(NP // 2 - 1, 0, True, False)
            pair(NP // 2 - 1, 1, False, False)

        @block.tensor
        def _(pe):
            cnt = [0]

            def item_pro(name, fn):
                k = pro(name)
                if k >= 2:
                    pe.wait_ge(emptied[k % 2], k // 2)
                fn(ring[k % 2]).then_inc(filled[k % 2], 1)

            def tr4(blocks, idn=None):
                def f(ps):
                    for j, a in enumerate(blocks):
                        w = a.shape[0]
                        last = pe.transpose(ps[:, j * w:(j + 1) * w], a, ident[0:w, 0:w])
                    return last
                return f

            def project(j, half):
                def f(ps):
                    parts = [(w, x, kt) for kt in range(KT) for w, x in ((pw_h, xr_h), (pw_l, xr_h), (pw_h, xr_l))]
                    for n, (w, x, kt) in enumerate(parts):
                        last = pe.matmul(ps[:], w[:, kt, j, :], x[:, kt, half * 512:half * 512 + 512],
                                         start=(n == 0), stop=(n == len(parts) - 1))
                    return last
                return f

            def v_back(half):
                return tr4([v_T[:, (4 * half + j) * P:(4 * half + j + 1) * P] for j in range(4)])

            def conv(slot, t0, t1):
                for t in range(t0, t1):
                    g = 64 * (t % 2)
                    last = pe.matmul(p_conv[g:g + 64, 0:128], kvb[:, t, :],
                                     conv_w[slot][:, :, :, t].rearrange("p a o -> p (a o)"),
                                     start=(t < 2), stop=(t >= CBS - 2), skip_group_check=True)
                return last

            pe.wait_ge(consts, 2)
            for kt in range(KT):
                for half in range(2):
                    if kt == 0:
                        pe.wait_ge(xr_ready, 4 * half + 4)
                    item_pro(f"xr{2 * kt + half}", tr4([xr[:, 4 * half + j, kt * P:kt * P + P] for j in range(4)]))
            pe.wait_ge(pos_in, 32)
            for m in range(4):
                item_pro(f"pos{m}", tr4([pos_raw[:, 8 * m + 2 * j:8 * m + 2 * j + 2, :].rearrange("p h d -> p (h d)") for j in range(4)]))
            pe.wait_ge(x_split, 4)
            pe.wait_ge(w_split, 4)
            for half in range(2):
                item_pro(f"k{half}", project(1, half))
            pe.wait_ge(wsum, 2)
            pe.matmul(p_y[:, 0:2], ones[:], wstat[:, 0:2], start=True, stop=True).then_inc(wtot, 1)
            for half in range(2):
                item_pro(f"v{half}", project(2, half))
            pe.wait_ge(xn_ready, T)
            for kt in range(KT):
                for half in range(2):
                    item_pro(f"xn{2 * kt + half}", tr4([xc[:, 4 * half + j, kt * P:kt * P + P] for j in range(4)]))
            for half in range(2):
                item_pro(f"q{half}", project(0, half))
            for half in range(2):
                item_pro(f"t{half}", v_back(half))
            pe.wait_ge(small_in, 64)
            for g in range(2):
                def f(ps, g=g):
                    for j in range(4):
                        for kt in range(KT):
                            last = pe.matmul(ps[:, j * 96:(j + 1) * 96], xr_T[:, kt, (4 * g + j) * P:(4 * g + j + 1) * P],
                                             wcomb[:, kt], start=(kt == 0), stop=(kt == KT - 1))
                    return last
                item_pro(f"g{g}", f)
            pe.wait_ge(wq_ready, 1)
            for kt in range(KT):
                for half in range(2):
                    item_pro(f"w1{2 * kt + half}", tr4([w1_s[:, 4 * half + j, kt * P:kt * P + P] for j in range(4)]))
            pe.wait_ge(w2q_ready, 2)
            for m in range(4):
                item_pro(f"w2{m}", tr4([w2_s[:, e, (2 * m + f) * P:(2 * m + f + 1) * P] for f in range(2) for e in range(2)]))
            for g in range(2):
                for b in range(2):
                    pe.wait_ge(emptied[b], pro(f"w2{2 + b}") // 2 + 1)
                for ft in range(FT):
                    def f(ps, g=g, ft=ft):
                        for kt in range(KT):
                            for x in (xn_h, xn_l):
                                last = pe.matmul(ps[:], w1_T[:, kt, ft * P:(ft + 1) * P], x[:, kt, g * 512:g * 512 + 512],
                                                 start=(kt == 0 and x is xn_h), stop=(kt == KT - 1 and x is xn_l))
                        return last
                    item_pro(f"h{g}_{ft}", f)
                for j in range(2):
                    def f(ps, g=g, j=j):
                        for m in range(2):
                            for ft in range(FT):
                                if j == m == 0:
                                    pe.wait_ge(g_split, FT * g + ft + 1)
                                for x in (g_h, g_l):
                                    last = pe.matmul(ps[:, m * DIM:(m + 1) * DIM], x[:, ft, (2 * j + m) * P:(2 * j + m + 1) * P],
                                                     w2_T[:, ft], start=(ft == 0 and x is g_h), stop=(ft == FT - 1 and x is g_l))
                        return last
                    item_pro(f"f{g}_{j}", f)
            pe.wait_ge(bd_ready, 4)
            pe.wait_ge(bd2_ready, 4)
            pe.wait_ge(conv_in[0], 64)
            conv(0, 0, CBS).then_inc(conv_done, 1)

            def pair(i, s, prep):
                pr = Pair(i, s)
                p, nx = pr.p, pr.nxt

                def item(name, fn):
                    b = int(name[1])
                    ring_wait_free(pe, b, pr.ordinal(name) if prep else pr.ordinal_last(name))
                    fn(ring[b]).then_inc(filled[b], 1)

                def sim(b):
                    if b == 1:
                        pe.wait_ge(y_added, p * 4 + FREE_BANK)
                    pe.wait_ge(sim_read, p * T + (b + 1))
                    lo = (b - 1) * W if b else 0
                    for h in range(2):
                        last = pe.matmul(p_sim[b % 2][:, h * 256 + (0 if b else W):(h + 1) * 256], q_T[s][:, b * P:(b + 1) * P],
                                         kz[s][h][:, lo:(b + 1) * W], start=True, stop=True)
                    last.then_inc(sim_done, 1)

                def turn_probs(b):
                    pe.wait_ge(p_ready, p * T + (b + 1))
                    pe.wait_ge(pt_evac, p * T + (b + FREE_BANK))
                    for h in range(2):
                        for c in range(0 if b else 1, 2):
                            last = pe.transpose(p_pt[:, (2 * h + c) * P:(2 * h + c + 1) * P],
                                                prob[:, b % 4, h, c * W:(c + 1) * W], ident[:])
                    last.then_inc(pt_done, 1)

                def pv(b):
                    pe.wait_ge(pt_evac, p * T + (b + 1 + FREE_BANK))
                    for c in range(0 if b else 1, 2):
                        for h in range(2):
                            last = pe.matmul(p_o[64 * h:64 * h + 64, (b % 4) * P:(b % 4 + 1) * P],
                                             v_tok[s][:, b - 1 + c, 64 * h:64 * h + 64], prob_T[:, b % 2, 2 * h + c, :],
                                             start=False, stop=True, skip_group_check=True)
                    last.then_inc(pv_done, 1)

                def comp_out(half):
                    pe.wait_ge(o_evac, p * 2 + (half + FREE_BANK))
                    pe.matmul(p_o[:], cv_bd[:], pc_T[:, half * 512:half * 512 + 512], start=True, stop=False,
                              skip_group_check=True)

                def y(j):
                    half = j // 2
                    if j % 2 == 0:
                        pe.wait_ge(o_evac, p * 2 + (half + 1 + FREE_BANK))
                        pe.wait_ge(outw_in[s], (i + 1) * 16)
                    bank_y = p_y
                    if j < 3:
                        pe.wait_ge(y_added, p * 4 + (j + FREE_BANK))
                    else:
                        pe.wait_ge(sim_read, p * T + (T + FREE_SIM))
                        bank_y = p_sim[1]
                    for m in range(2):
                        c = (2 * (j % 2) + m) * P
                        last = pe.matmul(bank_y[:, m * DIM:(m + 1) * DIM], o_T[:, half, c:c + P], out_w[s][:], start=True, stop=True)
                    last.then_inc(y_done, 1)

                pe.wait_ge(conv_evac, p + 1)
                for h in range(2):
                    pe.matmul(ck_ps[64 * h:64 * h + 64, 16 * h:16 * h + 16], conv_s[:, 0:64], sel[:, 16 * h:16 * h + 16],
                              start=True, stop=True, skip_group_check=True)
                pe.matmul(cv_ps, sel[:, 32:64], conv_s[:, 64:128], start=True, stop=True,
                          skip_group_check=True).then_inc(sel_done, 1)
                sim(0)
                if prep:
                    pe.wait_ge(w_split, p * 4 + 8)
                    item("k0", project(1, 0))
                    item("k1", project(1, 1))
                pe.wait_ge(ckcv, p + 1)
                for b in range(T):
                    last = pe.matmul(csim_ps[:, b].rearrange("p h n -> p (h n)"), q_T[s][:, b * P:(b + 1) * P], ck_bd[:],
                                     start=True, stop=True, skip_group_check=True)
                last.then_inc(csim_done, 1)
                if prep:
                    item("v0", project(2, 0))
                    item("v1", project(2, 1))
                sim(1)
                if prep:
                    item("q0", project(0, 0))
                    item("q1", project(0, 1))
                turn_probs(0)
                sim(2)
                pe.wait_ge(pc_ready, p + 1)
                for half in range(2):
                    def f(ps, half=half):
                        for j in range(4):
                            last = pe.transpose(ps[0:32, j * P:(j + 1) * P],
                                                c_p[:, 4 * half + j].rearrange("p h n -> p (h n)"), ident[:])
                        return last
                    item(f"c{half}", f)
                for half in range(2):
                    pe.wait_ge(emptied[half], pr.ordinal(f"c{half}") if prep else pr.ordinal_last(f"c{half}"))
                comp_out(0)
                for b in range(T):
                    if b:
                        turn_probs(b)
                        if b + 2 < T:
                            sim(b + 2)
                    if prep:
                        if b == 0:
                            for half in range(2):
                                pe.wait_ge(emptied[half], pr.ordinal(f"v{half}"))
                                item(f"t{half}", v_back(half))
                        else:
                            if b == 1:
                                pe.wait_ge(bd_ready, p * 4 + 8)
                                pe.wait_ge(bd2_ready, p * 4 + 8)
                                pe.wait_ge(conv_in[nx], (pr.nxt_use + 1) * 64)
                                pe.wait_ge(csim_read, p + 1)
                            conv(nx, 8 * (b - 1), 8 * b)
                    if b == 4:
                        comp_out(1)
                    pv(b)
                    if b in (5, 6):
                        y(b - 5)
                if prep:
                    conv(nx, 56, CBS).then_inc(conv_done, 1)
                y(2)
                y(3)

            pe.wait_ge(consts, 5)
            with pe.Fori(0, NP // 2 - 1) as i:
                pair(i, 0, True)
                pair(i, 1, True)
            pair(NP // 2 - 1, 0, True)
            pair(NP // 2 - 1, 1, False)

        @block.scalar
        def _(act):
            def item_pro(name):
                k = pro(name)
                assert k % 2 == 0
                act.wait_ge(filled[0], k // 2 + 1)
                return ring[0]

            def take(name, slot, ps, ins_wait=None):
                if name == "k0":
                    act.copy(kz[slot][0][0:64, 0:512], ps[0:64, :])
                    return act.copy(kz[slot][1][64:128, 0:512], ps[64:128, :])
                if name == "v0":
                    return act.copy(v_T[:, 0:512], ps[:])
                if name == "q0":
                    return act.mul(q_T[slot][:, 0:512], ps[:], SCALE)
                if name == "t0":
                    return act.copy(v_tok[slot][:, 0:4].rearrange("p b n -> p (b n)"), ps[:])
                return act.copy(pc_T[0:32, 0:512], ps[0:32, :])

            for r in range(2):
                act.wait_ge(rt_in, r + 1)
                act.activation(stat[:, 4 + r], stat[:, 2 + r], ACT.Sqrt).then_inc(rt_out, 1)
            act.wait_ge(rms_in, 16)
            for kt in range(KT):
                ps = item_pro(f"xr{2 * kt}")
                act.activation(xr_T[:, kt, 0:512], ps[:], ACT.Copy, scale=rms_c[:, kt:kt + 1]).then_inc(xr_T_ready, 1)
                act.activation(xr_h[:, kt, 0:512], ps[:], ACT.Copy, scale=rms_c[:, kt:kt + 1]).then_inc(emptied[0], 1)
            for m in range(4):
                wait_filled(act, pro(f"pos{m}"))
                act.copy(pos_T[:, 4 * m:4 * m + 4].rearrange("p a b c -> p (a b c)"), ring[m % 2][:]).then_inc(emptied[m % 2], 1)

            def abs_sums(n, w_s):
                act.wait_ge(w12_in, 32)
                for half in range(2):
                    part = w_s[:, 4 * half:4 * half + 4] if n == 0 else w_s[:, half:half + 1]
                    if n + half:
                        act.wait_ge(wabs, 2 * n + half)
                    act.activation(w_abs.rearrange("p (a b) -> p a b", a=part.shape[1]), part, ACT.Abs,
                                   accum_out=wstat[:, 4 + 2 * n + half:5 + 2 * n + half]).then_inc(wabs, 1)

            act.wait_ge(consts, 3)
            abs_sums(0, w1_s)
            take("k0", 0, item_pro("k0")).then_inc(emptied[0], 1)
            abs_sums(1, w2_s)
            take("v0", 0, item_pro("v0")).then_inc(emptied[0], 1)
            for kt in range(KT):
                for half in range(2):
                    wait_filled(act, pro(f"xn{2 * kt + half}"))
                    act.copy(xn_h[:, kt, 512 * half:512 * half + 512], ring[half][:]).then_inc(xn_h_ready, 1)
            for name in ("q0", "t0"):
                take(name, 0, item_pro(name)).then_inc(emptied[0], 1)
            ps = item_pro("g0")
            act.copy(sig[:, 0:4].rearrange("p b n -> p (b n)"), ps[:, 0:384]).then_inc(emptied[0], 1)
            for kt in range(KT):
                act.activation(w1_T[:, kt, 0:512], item_pro(f"w1{2 * kt}")[:], ACT.Copy, bias=-ROUND).then_inc(emptied[0], 1)
            for m in (0, 2):
                act.activation(w2_T[:, 2 * m:2 * m + 2].rearrange("p f e -> p (f e)"), item_pro(f"w2{m}")[:],
                               ACT.Copy, bias=-ROUND).then_inc(emptied[0], 1)
            act.wait_ge(glog, 1)
            act.activation(sig[:], sig[:], ACT.Exp, scale=-1.0).then_inc(gexp, 1)
            act.wait_ge(small_in, 64)
            for g in range(2):
                for ft in range(FT):
                    k = pro(f"h{g}_{ft}")
                    n = FT * g + ft
                    wait_filled(act, k)
                    if n >= 2:
                        act.wait_ge(g_split, n - 1)
                    if ft % 2 == 0:
                        act.activation(g_h[:, ft], ring[k % 2][:], ACT.Gelu, bias=b1_c[:, ft:ft + 1]).then_inc(gh_ready, 1)
                    act.activation(g_f[:, ft % 2], ring[k % 2][:], ACT.Gelu, bias=b1_c[:, ft:ft + 1]).then_inc(emptied[k % 2], 1)

            def pair(i, s, prep):
                pr = Pair(i, s)
                p = pr.p

                def evac(name):
                    act.wait_ge(filled[0], pr.ordinal(name) if prep else pr.ordinal_last(name))
                    take(name, s if name == "c0" else pr.nxt, ring[0]).then_inc(emptied[0], 1)

                def exps(b):
                    lo = 0 if b else W
                    act.wait_ge(sim_read, p * T + (b + 1 + FREE_SIM))
                    act.wait_ge(pt_done, p * T + (b + 1))
                    for h in range(2):
                        act.activation(prob[:, b % 4, h, lo:], s_neg[:, b % 2, h, lo:], ACT.Exp, bias=ncol[:, b, h:h + 1],
                                       scale=-1.0, accum_out=lsum[:, b, h:h + 1]).then_inc(exp_done, 1)

                exps(0)
                if prep:
                    evac("k0")
                act.wait_ge(cs_ready, p + 1)
                act.activation(c_e[:], c_s[:], ACT.Exp).then_inc(ce_ready, 1)
                if prep:
                    evac("v0")
                exps(1)
                if prep:
                    evac("q0")
                evac("c0")
                for b in range(T):
                    act.wait_ge(pt_done, p * T + (b + 1 + FREE_PT))
                    act.wait_ge(pv_done, p * T + (b - 1 + FREE_PV))
                    turned = p_pt[:].rearrange("p (a n) -> p a n", a=4)
                    which = slice(0, 4) if b else slice(1, 4, 2)
                    act.copy(prob_T[:, b % 2, which], turned[:, which]).then_inc(pt_evac, 1)
                    if b + 2 < T:
                        exps(b + 2)
                    if b == 0 and prep:
                        evac("t0")

            act.wait_ge(consts, 5)
            with act.Fori(0, NP // 2 - 1) as i:
                pair(i, 0, True)
                pair(i, 1, True)
            pair(NP // 2 - 1, 0, True)
            pair(NP // 2 - 1, 1, False)

        @block.vector
        def _(dve):
            n = [0]

            def link(ins):
                n[0] += 1
                ins.then_inc(dch, 1)
                dve.wait_ge(dch, n[0])

            def item_pro(name):
                k = pro(name)
                dve.wait_ge(filled[k % 2], k // 2 + 1)
                return ring[k % 2]

            def over(a):
                return a.unsqueeze(2).broadcast_to([P, T, DIM])

            for b in range(T):
                if b % 2 == 0:
                    dve.wait_ge(x_in[b // 2], 16)
                last = dve.bn_stats(out=bn[:, b], in_=acc[:, b])
            link(last)
            for b in range(T):
                last = dve.bn_aggr(out=mv[:, b], in_=bn[:, b])
            link(last)
            var = mv[:, :, 1]
            dve.tensor_scalar(stat[:, 2], var, LN_EPS, None, ALU.add).then_inc(rt_in, 1)
            dve.wait_ge(rt_out, 1)
            link(dve.reciprocal(stat[:, 6], stat[:, 4]))
            link(dve.tensor_tensor(out=stat[:, 0], in0=stat[:, 6], in1=stat[:, 6], op=ALU.mult))
            link(dve.tensor_tensor(out=stat[:, 1], in0=stat[:, 0], in1=var, op=ALU.mult))
            dve.tensor_scalar(stat[:, 3], stat[:, 1], RMS_EPS, None, ALU.add).then_inc(rt_in, 1)
            dve.wait_ge(rt_out, 2)
            link(dve.reciprocal(stat[:, 7], stat[:, 5]))
            link(dve.tensor_tensor(out=stat[:, 0], in0=stat[:, 7], in1=stat[:, 6], op=ALU.mult))
            for b in range(T):
                dve.tensor_scalar(xr[:, b], acc[:, b], mv[:, b, 0:1], stat[:, 0, b:b + 1], ALU.subtract, ALU.mult).then_inc(xr_ready, 1)

            def evac_pro(name, dst, kt=None):
                ps = item_pro(name)
                if kt is None:
                    dve.tensor_copy(dst, ps[:]).then_inc(emptied[1], 1)
                else:
                    dve.tensor_scalar(dst, ps[:], rms_c[:, kt:kt + 1], None, ALU.mult).then_inc(emptied[1], 1)

            def take(name, slot, ps):
                if name == "k1":
                    dve.tensor_copy(kz[slot][0][0:64, 512:1024], ps[0:64, :])
                    return dve.tensor_copy(kz[slot][1][64:128, 512:1024], ps[64:128, :])
                if name == "v1":
                    return dve.tensor_copy(v_T[:, 512:1024], ps[:])
                if name == "q1":
                    return dve.tensor_scalar(q_T[slot][:, 512:1024], ps[:], SCALE, None, ALU.mult)
                if name == "t1":
                    return dve.tensor_copy(v_tok[slot][:, 4:8].rearrange("p b n -> p (b n)"), ps[:])
                return dve.tensor_copy(pc_T[0:32, 512:1024], ps[0:32, :])

            def build(q, kv, ps):
                for h in range(2):
                    r = slice(64 * h, 64 * h + 64)
                    pos = pos_T[r, bass.ds(q, 1), kv].rearrange("p a t -> p (a t)").unsqueeze(2).broadcast_to([64, CBS, NB // 2])
                    c = 32 * kv + 16 * h + NB // 2
                    dve.tensor_tensor(out=kvb[r, :, c:c + NB // 2], in0=ps[r, :].rearrange("p (n t) -> p t n", t=CBS),
                                      in1=pos, op=ALU.add).then_inc(bd2_ready, 1)

            dve.wait_ge(rms_in, 16)
            for kt in range(KT):
                ps = item_pro(f"xr{2 * kt + 1}")
                dve.tensor_scalar(xr_T[:, kt, 512:1024], ps[:], rms_c[:, kt:kt + 1], None, ALU.mult).then_inc(xr_T_ready, 1)
                dve.tensor_scalar(xr_h[:, kt, 512:1024], ps[:], rms_c[:, kt:kt + 1], None, ALU.mult).then_inc(emptied[1], 1)
            dve.wait_ge(xr_T_ready, 4)
            for b in range(2):
                dve.wait_ge(emptied[b], pro(f"xr{2 + b}") // 2 + 1)
            for half in range(2):
                for kt in range(KT):
                    c = slice(512 * half, 512 * half + 512)
                    dve.tensor_tensor(out=xr_l[:, kt, c], in0=xr_T[:, kt, c], in1=xr_h[:, kt, c], op=ALU.subtract).then_inc(x_split, 1)
            for b in range(T):
                dve.tensor_scalar(xc[:, b], acc[:, b], mv[:, b, 0:1], stat[:, 6, b:b + 1], ALU.subtract, ALU.mult).then_inc(xn_ready, 1)
            dve.wait_ge(consts, 3)
            for half in range(2):
                dve.wait_ge(emptied[half], pro(f"pos{2 + half}") // 2 + 1)

            def prep0(name):
                ps = item_pro(name)
                if name in ("k1", "v1"):
                    build(0, int(name == "v1"), ps)
                take(name, 0, ps).then_inc(emptied[1], 1)

            prep0("k1")
            dve.wait_ge(wabs, 4)
            for j in range(2):
                dve.tensor_tensor(out=wstat[:, j:j + 1], in0=wstat[:, 4 + 2 * j:5 + 2 * j], in1=wstat[:, 5 + 2 * j:6 + 2 * j],
                                  op=ALU.add).then_inc(wsum, 1)
            dve.wait_ge(wtot, 1)
            link(dve.tensor_scalar(wstat[:, 2:4], p_y[:, 0:2], 1.0 / (DFF * DIM), Q_EPS, ALU.mult, ALU.max))
            dve.reciprocal(wstat[:, 8:10], wstat[:, 2:4]).then_inc(wscale, 1)
            prep0("v1")
            dve.wait_ge(wscale, 1)
            link(dve.tensor_scalar(w1_s, w1_s, wstat[:, 8:9], 1.0, ALU.mult, ALU.min))
            dve.tensor_scalar(w1_s, w1_s, -1.0, ROUND, ALU.max, ALU.add).then_inc(wq_ready, 1)
            for kt in range(KT):
                for half in range(2):
                    ps = item_pro(f"xn{2 * kt + half}")
                    c = slice(512 * half, 512 * half + 512)
                    dve.wait_ge(xn_h_ready, 2 * kt + half + 1)
                    dve.tensor_tensor(out=xn_l[:, kt, c], in0=ps[:], in1=xn_h[:, kt, c], op=ALU.subtract).then_inc(emptied[half], 1)
            prep0("q1")
            prep0("t1")
            dve.wait_ge(small_in, 64)
            ps = item_pro("g1")
            dve.tensor_copy(sig[:, 4:8].rearrange("p b n -> p (b n)"), ps[:, 0:384]).then_inc(emptied[1], 1)
            for b in range(2):
                dve.wait_ge(emptied[b], pro(f"g{b}") // 2 + 1)
            dve.tensor_tensor(out=sig[:], in0=sig[:], in1=bc_r[:].unsqueeze(1).broadcast_to([P, T, 3 * H]), op=ALU.add).then_inc(glog, 1)
            for kt in range(KT):
                ps = item_pro(f"w1{2 * kt + 1}")
                dve.tensor_scalar(w1_T[:, kt, 512:1024], ps[:], -ROUND, None, ALU.add).then_inc(emptied[1], 1)
            for m in (1, 3):
                ps = item_pro(f"w2{m}")
                dve.tensor_scalar(w2_T[:, 2 * m:2 * m + 2].rearrange("p f e -> p (f e)"), ps[:], -ROUND, None, ALU.add).then_inc(emptied[1], 1)
            dve.wait_ge(b2_added, 4)
            for g in range(2):
                for ft in range(FT):
                    n_h = FT * g + ft
                    dve.wait_ge(emptied[ft % 2], pro(f"h{g}_{ft}") // 2 + 1)
                    if ft % 2:
                        link(dve.tensor_copy(g_h[:, ft], g_f[:, ft % 2]))
                    else:
                        dve.wait_ge(gh_ready, n_h // 2 + 1)
                    dve.tensor_tensor(out=g_l[:, ft], in0=g_f[:, ft % 2], in1=g_h[:, ft], op=ALU.subtract).then_inc(g_split, 1)
                for j in range(2):
                    ps = item_pro(f"f{g}_{j}")
                    a = acc[:, 4 * g + 2 * j:4 * g + 2 * j + 2].rearrange("p b c -> p (b c)")
                    dve.tensor_tensor(out=a, in0=a, in1=ps[:], op=ALU.add).then_inc(emptied[pro(f"f{g}_{j}") % 2], 1)

            def conv_out(q, slot, use):
                dve.wait_ge(conv_done, q + 1)
                dve.wait_ge(bias_in[slot], (use + 1) * 64)
                dve.tensor_tensor(out=conv_s[:], in0=p_conv[:, 0:128], in1=conv_b[slot][:], op=ALU.add).then_inc(conv_evac, 1)

            dve.wait_ge(gexp, 1)
            link(dve.tensor_scalar(sig[:], sig[:], 1.0, None, ALU.add))
            link(dve.reciprocal(sig[:], sig[:]))
            sg = sig[:].rearrange("p b (q h k) -> p q b h k", h=2, k=3)
            dve.tensor_tensor(out=gate[:, :, 0], in0=sg[:, :, :, :, 0], in1=sg[:, :, :, :, 1], op=ALU.add).then_inc(gates, 1)
            dve.tensor_copy(gate[:, :, 1], sg[:, :, :, :, 2]).then_inc(gates, 1)
            conv_out(0, 0, 0)
            dve.wait_ge(gates, 2)

            CCHAIN, LCHAIN = 5, 8

            def pair(i, s, prep):
                pr = Pair(i, s)
                p = pr.p
                c, l = [0], [0]

                def link_c(ins):
                    c[0] += 1
                    ins.then_inc(cchain, 1)
                    dve.wait_ge(cchain, p * CCHAIN + c[0])

                def evac(name):
                    dve.wait_ge(filled[1], pr.ordinal(name) if prep else pr.ordinal_last(name))
                    if name in ("k1", "v1"):
                        build(p + 1, int(name == "v1"), ring[1])
                    take(name, s if name == "c1" else pr.nxt, ring[1]).then_inc(emptied[1], 1)

                def scores(b):
                    c0 = 0 if b else 1
                    dve.wait_ge(sim_done, p * T + (b + 1))
                    dve.wait_ge(exp_done, (p * T + b) * 2 + 2)
                    dve.sem_inc(step_begun, 1)
                    for h in range(2):
                        ins = dve.tensor_tensor_reduce(
                            out=s_neg[:, b % 2, h, c0 * W:].rearrange("p (c j) -> p c j", j=W),
                            in0=p_sim[b % 2][:, h * 256 + c0 * W:(h + 1) * 256].rearrange("p (c j) -> p c j", j=W),
                            in1=mask_l[:, c0:], scale=-1.0, scalar=-NEG * 2, op0=ALU.add, op1=ALU.min,
                            accum_out=ncol[:, b, h:h + 1])
                    ins.then_inc(sim_read, 1)

                def row_scale(b):
                    l[0] += 1
                    dve.wait_ge(exp_done, (p * T + b) * 2 + (2 + FREE_EXP))
                    dve.reciprocal(rinv[:, b], lsum[:, b]).then_inc(lchain, 1)
                    dve.wait_ge(lchain, p * LCHAIN + l[0])
                    dve.tensor_tensor(out=rloc[:, b], in0=rinv[:, b], in1=gate_p[:, 0, b], op=ALU.mult).then_inc(r_ready, 1)

                def y_add(j):
                    dve.wait_ge(y_done, p * 4 + (j + 1 + FREE_Y))
                    dve.wait_ge(y_added, p * 4 + (j + FREE_BANK))
                    a = acc[:, 2 * j:2 * j + 2].rearrange("p b c -> p (b c)")
                    dve.tensor_tensor(out=a, in0=a, in1=(p_y if j < 3 else p_sim[1])[:], op=ALU.add).then_inc(y_added, 1)

                def o_out(half):
                    dve.wait_ge(pv_done, p * T + (4 * half + 4 + FREE_PV))
                    dve.wait_ge(y_done, p * 4 + (2 * half - 2 + FREE_Y))
                    dve.tensor_copy(o_T[:, half], p_o[:]).then_inc(o_evac, 1)

                dve.wait_ge(sel_done, p + 1)
                for h in range(2):
                    dve.tensor_copy(ck_bd[64 * h:64 * h + 64, 16 * h:16 * h + 16], ck_ps[64 * h:64 * h + 64, 16 * h:16 * h + 16])
                dve.tensor_tensor(out=cv_bd[0:32].rearrange("p (h o) -> p h o", h=2), in0=cv_ps.unsqueeze(1).broadcast_to([32, 2, DH]),
                                  in1=block_m[:], op=ALU.mult).then_inc(ckcv, 1)
                link_c(dve.tensor_copy(gate_p[:].rearrange("p a b c -> p (a b c)"), gate[:, bass.ds(p, 1)].rearrange("p q a b c -> p (q a b c)")))
                scores(0)
                if prep:
                    evac("k1")
                row_scale(0)
                dve.wait_ge(csim_done, p + 1)
                dve.tensor_tensor(out=c_s[:], in0=csim_ps, in1=mask_c[:].unsqueeze(2).broadcast_to([P, T, 2, NB]), op=ALU.add).then_inc(csim_read, 1)
                dve.wait_ge(csim_read, p + 1)
                cs2 = c_s[:].rearrange("p b h n -> p (b h) n")
                link_c(dve.tensor_reduce(c_m[:], cs2, AX.X, ALU.max))
                dve.tensor_tensor(out=cs2, in0=cs2, in1=c_m[:].unsqueeze(2).broadcast_to([P, 2 * T, NB]), op=ALU.subtract).then_inc(cs_ready, 1)
                if prep:
                    evac("v1")
                scores(1)
                dve.wait_ge(ce_ready, p + 1)
                ce2 = c_e[:].rearrange("p b h n -> p (b h) n")
                link_c(dve.tensor_reduce(c_l[:], ce2, AX.X, ALU.add))
                link_c(dve.reciprocal(c_r[:], c_l[:]))
                link_c(dve.tensor_tensor(out=c_g[:], in0=c_r[:], in1=gate_p[:, 1].rearrange("p b h -> p (b h)"), op=ALU.mult))
                dve.tensor_tensor(out=c_p[:].rearrange("p b h n -> p (b h) n"), in0=ce2,
                                  in1=c_g[:].unsqueeze(2).broadcast_to([P, 2 * T, NB]), op=ALU.mult).then_inc(pc_ready, 1)
                row_scale(1)
                if prep:
                    evac("q1")
                evac("c1")
                for b in range(T):
                    if b == 4:
                        o_out(0)
                    if b + 2 < T:
                        scores(b + 2)
                        row_scale(b + 2)
                    if b == 0 and prep:
                        evac("t1")
                    if b in (6, 7):
                        y_add(b - 6)
                o_out(1)
                if prep:
                    conv_out(p + 1, pr.nxt, pr.nxt_use)
                y_add(2)
                y_add(3)
                assert c[0] == CCHAIN and l[0] == LCHAIN, (c, l)

            dve.wait_ge(consts, 5)
            with dve.Fori(0, NP // 2 - 1) as i:
                pair(i, 0, True)
                pair(i, 1, True)
            pair(NP // 2 - 1, 0, True)
            pair(NP // 2 - 1, 1, False)


_INS = ["L0_attn_inp", "L0_attn_rms_w", "L0_attn_w_qkv", "L0_attn_k_pos", "L0_attn_v_pos", "L0_attn_kc_w",
        "L0_attn_kc_b", "L0_attn_vc_w", "L0_attn_vc_b", "L0_attn_w_comb", "L0_attn_b_comb", "L0_attn_w_out",
        "L0_ffn_w1", "L0_ffn_b1", "L0_ffn_w2", "L0_ffn_b2"]


def kernel(**inputs):
    import numpy as _np
    import concourse.bacc as _bacc
    from concourse import mybir as _mybir
    from concourse.bass_utils import run_bass_kernel_spmd as _run

    nc = _bacc.Bacc("TRN2", target_bir_lowering=False, num_devices=1)
    arrays, args = {}, []
    for name in _INS:
        a = _np.ascontiguousarray(inputs[name])
        arrays[f"in_{name}_dram"] = a
        args.append(nc.dram_tensor(f"in_{name}_dram", a.shape, _mybir.dt.from_np(a.dtype), kind="ExternalInput").ap())
    args.append(nc.dram_tensor("out_0_dram", (1, S, DIM), F32, kind="ExternalOutput").ap())
    layer(nc, *args)
    r = _run(nc, [arrays], core_ids=[0])
    return r.results[0]["out_0_dram"]
```

```python
from contextlib import ExitStack

import concourse.bass as bass
from concourse import mybir

F32 = mybir.dt.float32
F32R = mybir.dt.float32r
ALU = mybir.AluOpType
ACT = mybir.ActivationFunctionType
AX = mybir.AxisListType

P = 128
S, DIM, H, DH = 1024, 256, 32, 64
W = 128
CBS = 64
NB = S // CBS
T = S // P
KT = DIM // P
NP = H // 2
DFF = 1024
FT = DFF // P
SCALE = DH ** -0.5
NEG = -1e30
LN_EPS, RMS_EPS, Q_EPS = 1e-5, 1.1920929e-07, 1e-8
WARM = 18
ROUND = 1.5 * 2 ** 23

PRO_ITEMS = ([f"{n}{j}" for n in ("xr", "pos") for j in range(4)] + ["k0", "k1", "v0", "v1"]
             + [f"xn{j}" for j in range(4)] + ["t0", "t1", "g0", "g1"]
             + [f"{n}{j}" for n in ("w1", "w2") for j in range(4)])
FFN_ITEMS = [f"h{g}_{f}" for g in range(2) for f in range(FT)]
FFN_OUT = [f"f{g}_{j}" for g in range(2) for j in range(2)]
ORDER = PRO_ITEMS + [x for g in range(2) for x in FFN_ITEMS[g * FT:(g + 1) * FT] + FFN_OUT[g * 2:g * 2 + 2]] + ["q0", "q1"]
RING0 = len(ORDER)
PAIR_ITEMS = ["k0", "k1", "v0", "v1", "q0", "q1", "c0", "c1", "t0", "t1"]
RING_PER_PAIR = len(PAIR_ITEMS)
assert RING0 % 2 == 0 and all(int(x[-1]) % 2 == n % 2 for n, x in enumerate(ORDER))


def layer(nc, inp, rms_w, w_qkv, k_pos, v_pos, kc_w, kc_b, vc_w, vc_b, w_comb, b_comb, w_out,
          w1, b1, w2, b2, out):
    with ExitStack() as ctx:
        def sb(name, shape, dtype=F32, at=ctx):
            return at.enter_context(nc.sbuf_tensor(name, shape, dtype))

        def sem(name):
            return ctx.enter_context(nc.semaphore(name))

        acc = sb("acc", [P, T, DIM])
        xr_h = sb("xr_h", [P, KT, S], F32R)
        xr_l = sb("xr_l", [P, KT, S], F32R)
        pw_h = sb("pw_h", [P, KT, 3, P], F32R)
        pw_l = sb("pw_l", [P, KT, 3, P], F32R)
        pos_T = sb("pos_T", [P, NP, 2, CBS])
        with ExitStack() as early:
            raw = sb("raw", [P, 8192], at=early)
        with ExitStack() as early:
            g_h = sb("g_h", [P, FT, 512], F32R, at=early)
            g_l = sb("g_l", [P, FT, 512], F32R, at=early)
        conv_w = [sb(f"conv_w{s}", [P, 2, DH, CBS]) for s in (1, 0)][::-1]
        proj_w = [sb(f"proj_w{s}", [P, KT, 3, P]) for s in range(2)]
        out_w = [sb(f"out_w{s}", [P, DIM]) for s in range(2)]
        conv_b = [sb(f"conv_b{s}", [P, P]) for s in range(2)]
        with ExitStack() as early:
            xn_h = sb("xn_h", [P, KT, S], F32R, at=early)
            xn_l = sb("xn_l", [P, KT, S], F32R, at=early)
        kqv1 = sb("kqv1", [P, 4, S])
        kz = [[sb(f"kz{s}{h}", [P, S]) for h in range(2)] for s in range(1)]
        kz.append([kqv1[:, 0], kqv1[:, 1]])
        q_T = [sb("q_T0", [P, S]), kqv1[:, 2]]
        v_T = sb("v_T", [P, S])
        v_tok = [sb("v_tok0", [P, T, P]), kqv1[:, 3].rearrange("p (t n) -> p t n", t=T)]
        kvb = sb("kvb", [P, CBS, 64])
        s_neg = sb("s_neg", [P, 2, 2, 2 * W])
        with ExitStack() as early:
            xr_xn = sb("xr_xn", [P, T, DIM], at=early)
            xr_T = sb("xr_T", [P, KT, S], at=early)
        with ExitStack() as early:
            w1_T = sb("w1_T", [P, KT, DFF], F32R, at=early)
            w2_T = sb("w2_T", [P, FT, DIM], F32R, at=early)
        prob = sb("prob", [P, 4, 2, 2 * W])
        turned_o = sb("turned_o", [P, 2, 2, 4 * P])
        prob_T = turned_o[:, 0].rearrange("p a (c n) -> p a c n", c=4)
        o_T = turned_o[:, 1]
        ncol = sb("ncol", [P, T, 2])
        lsum = sb("lsum", [P, T, 2])
        rinv = sb("rinv", [P, T, 2])
        rloc = sb("rloc", [P, T, 2])
        gate_p = sb("gate_p", [P, 2, T, 2])
        gate = sb("gate", [P, NP, 2, T, 2])
        c_s = sb("c_s", [P, T, 2, NB])
        c_e = sb("c_e", [P, T, 2, NB])
        c_f = sb("c_f", [P, T, 2 * NB])
        c_p = sb("c_p", [P, T, 3, 2 * NB], F32R)
        c_m = sb("c_m", [P, T * 2])
        c_l = sb("c_l", [P, T * 2])
        c_r = sb("c_r", [P, T * 2])
        c_g = sb("c_g", [P, T * 2])
        pc_T = sb("pc_T", [P, S], F32R)
        conv_s = sb("conv_s", [P, P])
        cs_T = sb("cs_T", [P, 2 * P])
        ck_bd = sb("ck_bd", [P, 2 * NB])
        cv_f = sb("cv_f", [P, P])
        cv_bd = sb("cv_bd", [P, P], F32R)
        ident = sb("ident", [P, P])
        sel = sb("sel", [P, 64])
        sel_v = sb("sel_v", [P, 3, 32])
        ones = sb("ones", [P, P])
        mask_l = sb("mask_l", [P, 2, W])
        mask_c = sb("mask_c", [P, T, NB])
        block_m = sb("block_m", [P, 2, DH])
        rms_c = sb("rms_c", [P, KT])
        b1_c = sb("b1_c", [P, FT])
        b2_r = sb("b2_r", [P, DIM])
        bc_r = sb("bc_r", [P, 3 * H])
        wcomb = sb("wcomb", [P, KT, 3 * H])
        stat = sb("stat", [P, 8, T])
        wstat = sb("wstat", [P, 12])
        unused = sb("unused", [P, 2])
        sig = sb("sig", [P, T, 3 * H])
        xr = xc = xr_xn
        w1_s = raw[:, 0:2048].rearrange("p (j c) -> p j c", j=FT)
        w2_s = raw[:, 2048:4096].rearrange("p (j f) -> p j f", j=2)
        pos_raw = raw[:, 4096:6144].rearrange("p (h d) -> p h d", h=H)
        w_abs = s_neg[:].rearrange("p a b c -> p (a b c)")
        
        g_f = [t[:, 512 * m:512 * m + 512] for t in (w_abs, v_T) for m in range(2)]
        bn = sb("bn", [P, T, 6])
        mv = sb("mv", [P, T, 2])

        bank = [ctx.enter_context(nc.psum_tensor(f"bank{n}", [P, 512], F32)) for n in range(8)]
        ring, p_conv, p_sim, p_pt, p_o, p_y = bank[0:2], bank[2], bank[3:5], bank[5], bank[6], bank[7]
        ck_ps = p_conv[:, 128:160]
        cv_ps = p_conv[0:96, 192:256]
        csim_ps = p_conv[:, 256:512].rearrange("p (j g h n) -> p g j h n", j=2, g=4, h=2)

        x_in = [sem(f"x_in{g}") for g in range(4)]
        rms_in, small_in, w12_in, pos_in = sem("rms_in"), sem("small_in"), sem("w12_in"), sem("pos_in")
        proj_in = [sem(f"proj_in{s}") for s in range(2)]
        conv_in = [sem(f"conv_in{s}") for s in range(2)]
        bias_in = [sem(f"bias_in{s}") for s in range(2)]
        outw_in = [sem(f"outw_in{s}") for s in range(2)]
        consts = sem("consts")
        xr_ready, xn_ready = sem("xr_ready"), sem("xn_ready")
        rt_in, rt_out = sem("rt_in"), sem("rt_out")
        dch = sem("dch")
        pch = sem("pch")
        wabs, wsum, wtot, wq_ready = sem("wabs"), sem("wsum"), sem("wtot"), sem("wq_ready")
        wscale, b2_added = sem("wscale"), sem("b2_added")
        glog, gexp, gates = sem("glog"), sem("gexp"), sem("gates")
        filled = [sem(f"ring_filled{n}") for n in range(2)]
        emptied = [sem(f"ring_emptied{n}") for n in range(2)]
        bd2_ready, bd_ready, conv_done, conv_evac = sem("bd2_ready"), sem("bd_ready"), sem("conv_done"), sem("conv_evac")
        csT_done, csT_evac = sem("csT_done"), sem("csT_evac")
        sel_done, ckcv, csim_done = sem("sel_done"), sem("ckcv"), sem("csim_done")
        csim_read, cs_ready, ce_ready, pc_ready = sem("csim_read"), sem("cs_ready"), sem("ce_ready"), sem("pc_ready")
        w_split = sem("w_split")
        xr_T_ready, x_split = sem("xr_T_ready"), [sem(f"x_split{n}") for n in range(2)]
        xn_h_ready, gh_ready, g_split = sem("xn_h_ready"), sem("gh_ready"), sem("g_split")
        cchain, lchain = sem("cchain"), sem("lchain")
        sim_done, sim_read, exp_done = sem("sim_done"), sem("sim_read"), sem("exp_done")
        r_ready, p_ready, pt_done, pt_evac = sem("r_ready"), sem("p_ready"), sem("pt_done"), sem("pt_evac")
        pv_done, o_evac, y_done, y_added = sem("pv_done"), sem("o_evac"), sem("y_done"), sem("y_added")
        step_begun, split_begun = sem("step_begun"), sem("split_begun")
        stored = sem("stored")

        FREE_SIM, FREE_EXP, FREE_PT, FREE_PV, FREE_Y, FREE_BANK = 2, 4, 4, 2, 3, 1

        def wait_filled(eng, k):
            eng.wait_ge(filled[k % 2], k // 2 + 1)

        def pro(name):
            return ORDER.index(name)

        class Pair:

            def __init__(self, i, s):
                self.i, self.s, self.p = i, s, i * 2 + s
                self.nxt = None if s == -1 else (1 - s)
                self.nxt_use = i + s

            def ordinal_last(self, name):
                return self.p * (RING_PER_PAIR // 2) + (RING0 // 2 + 1)

            def ordinal(self, name):
                return self.p * (RING_PER_PAIR // 2) + (RING0 // 2 + PAIR_ITEMS.index(name) // 2 + 1)

        def ring_wait_free(pe, b, ordinal):
            pe.wait_ge(emptied[b], ordinal - 1)

        block = ctx.enter_context(nc.Block())

        @block.sync
        def _(sp):
            def load_proj(q, s):
                for kt in range(KT):
                    sp.dma_start(proj_w[s][:, kt], w_qkv[kt * P:(kt + 1) * P].rearrange("c (j n) -> c j n", j=3)[:, :, bass.ds(q * P, P)]).then_inc(proj_in[s], 16)

            def load_conv(q, s):
                for kv, src in enumerate((kc_w, vc_w)):
                    for h in range(2):
                        sp.dma_start(conv_w[s][64 * h:64 * h + 64, kv],
                                     src[bass.ds(q * 2 + h, 1)].rearrange("a o i t -> (a i) o t")).then_inc(conv_in[s], 16)

            def load_bias(q, s):
                for kv, src in enumerate((kc_b, vc_b)):
                    for h in range(2):
                        r = 32 * kv + 16 * h
                        sp.dma_start(conv_b[s][r:r + 16, 64 * kv:64 * kv + 64],
                                     src[bass.ds(q * 2 + h, 1)].broadcast_to([16, DH])).then_inc(bias_in[s], 16)

            def load_outw(q, s):
                sp.dma_start(out_w[s][:], w_out[bass.ds(q * P, P)]).then_inc(outw_in[s], 16)

            for g in range(4):
                sp.dma_start(acc[:, 2 * g:2 * g + 2], inp[0, 256 * g:256 * g + 256].rearrange("(b p) c -> p b c", p=P)).then_inc(x_in[g], 16)
            sp.dma_start(rms_c[:], rms_w.rearrange("(k p) -> p k", p=P), allow_slow_non_contiguous=True).then_inc(rms_in, 16)
            load_proj(0, 0)
            for n, src in enumerate((k_pos, v_pos)):
                sp.dma_start(pos_raw[64 * n:64 * n + 64], src.rearrange("h t d -> t h d")).then_inc(pos_in, 16)
            sp.dma_start(w1_s, w1.rearrange("(j p) c -> p j c", p=P)).then_inc(w12_in, 16)
            sp.dma_start(w2_s, w2.rearrange("(j p) f -> p j f", p=P)).then_inc(w12_in, 16)
            sp.dma_start(b1_c[:], b1.rearrange("(f p) -> p f", p=P), allow_slow_non_contiguous=True).then_inc(small_in, 16)
            sp.dma_start(b2_r[:], b2.partition_broadcast(P)).then_inc(small_in, 16)
            sp.dma_start(bc_r[:], b_comb.partition_broadcast(P)).then_inc(small_in, 16)
            sp.dma_start(wcomb[:], w_comb.rearrange("(k p) n -> p k n", p=P)).then_inc(small_in, 16)
            load_conv(0, 0)
            sp.wait_ge(consts, 1)
            load_bias(0, 0)
            load_outw(0, 0)
            load_proj(1, 1)
            load_bias(1, 1)
            load_outw(1, 1)
            sp.wait_ge(filled[1], pro("f1_1") // 2 + 1)
            load_conv(1, 1)

            def pair(i, s):
                p = i * 2 + s
                sp.wait_ge(filled[1], p * (RING_PER_PAIR // 2) + (RING0 // 2 - 2))
                load_proj(p + 2, s)
                sp.wait_ge(conv_evac, p + 1)
                load_conv(p + 2, s)
                load_bias(p + 2, s)
                sp.wait_ge(y_done, p * 4 + (FREE_Y + 4))
                load_outw(p + 2, s)

            with sp.Fori(0, NP // 2 - 1) as i:
                pair(i, 0)
                pair(i, 1)
            for m in range(4):
                sp.wait_ge(y_added, 4 * (NP - 1) + m + 1 + FREE_BANK)
                sp.dma_start(out[0, 256 * m:256 * m + 256].rearrange("(b p) c -> p b c", p=P),
                             acc[:, 2 * m:2 * m + 2]).then_inc(stored, 16)
            sp.wait_ge(stored, 64)

        @block.gpsimd
        def _(pool):
            n = [0]

            def link(ins):
                n[0] += 1
                ins.then_inc(pch, 1)
                pool.wait_ge(pch, n[0])

            link(pool.memset(unused[:], 0.0))
            for s in range(2):
                link(pool.memset(conv_b[s][:], 0.0))
            pool.sem_inc(consts, 1)
            link(pool.memset(ident[:], 0.0))
            link(pool.affine_select(out=ident[:], in_=ident[:], compare_op=ALU.not_equal, fill=1.0, base=0,
                                    pattern=[[-1, P]], channel_multiplier=1))
            pool.sem_inc(consts, 1)
            link(pool.memset(ones[:], 1.0))

            def split_weights(slot, use, q):
                split_high(slot, use, 0)
                split_high(slot, use, 1)
                split_low(slot, q, 0)
                split_low(slot, q, 1)

            def split_high(slot, use, kt):
                if kt == 0:
                    pool.wait_ge(proj_in[slot], (use + 1) * 32)
                    pool.sem_inc(split_begun, 1)
                pool.tensor_copy(out=pw_h[:, kt], in_=proj_w[slot][:, kt]).then_inc(w_split, 1)

            def split_low(slot, q, kt):
                pool.wait_ge(w_split, q * 4 + (kt + 2))
                pool.tensor_tensor(out=pw_l[:, kt], in0=proj_w[slot][:, kt], in1=pw_h[:, kt], op=ALU.subtract).then_inc(w_split, 1)
                if kt == KT - 1:
                    pool.wait_ge(w_split, q * 4 + 4)

            link(pool.memset(kvb[:], 0.0))
            link(pool.memset(kz[0][0][64:128], 0.0))
            link(pool.memset(kz[0][1][0:64], 0.0))
            pool.sem_inc(consts, 1)
            split_weights(0, 0, 0)
            pool.wait_ge(xr_T_ready, 4)
            for b in range(2):
                pool.wait_ge(emptied[b], pro(f"xr{2 + b}") // 2 + 1)
            for kt in range(KT):
                pool.tensor_tensor(out=xr_l[:, kt, 512:1024], in0=xr_T[:, kt, 512:1024], in1=xr_h[:, kt, 512:1024],
                                   op=ALU.subtract).then_inc(x_split[1], 1)
            link(pool.memset(mask_l[:], 0.0))
            link(pool.memset(mask_c[:], 0.0))
            link(pool.memset(block_m[:], 1.0))
            link(pool.tensor_tensor(out=sel[:], in0=ident[:, 0:64], in1=ident[:, 64:128], op=ALU.add))
            link(pool.tensor_copy(out=sel_v[:], in_=sel[:, 32:64].unsqueeze(1).broadcast_to([P, 3, 32])))
            link(pool.affine_select(out=mask_l[:, 0], in_=mask_l[:, 0], compare_op=ALU.is_ge, fill=NEG, base=0,
                                    pattern=[[1, W]], channel_multiplier=-1))
            link(pool.affine_select(out=mask_l[:, 1], in_=mask_l[:, 1], compare_op=ALU.is_ge, fill=NEG, base=0,
                                    pattern=[[-1, W]], channel_multiplier=1))
            link(pool.affine_select(out=mask_c[:], in_=mask_c[:], compare_op=ALU.is_ge, fill=NEG, base=CBS - 1,
                                    pattern=[[-P, T], [CBS, NB]], channel_multiplier=-1))
            for part in range(3):
                for sign in (1, -1):
                    link(pool.affine_select(out=block_m[32 * part:32 * part + 32], in_=block_m[32 * part:32 * part + 32],
                                            compare_op=ALU.is_ge, fill=0.0, base=15 if sign < 0 else 0,
                                            pattern=[[-16 * sign, 2], [0, DH]], channel_multiplier=sign))
            link(pool.memset(ck_bd[:], 0.0))
            link(pool.memset(cv_f[:], 0.0))
            link(pool.tensor_copy(out=cv_bd[:], in_=cv_f[:]))
            pool.tensor_copy(out=pc_T[:].rearrange("p (b n) -> p b n", b=T), in_=cv_f[:].unsqueeze(1).broadcast_to([P, T, P])).then_inc(consts, 1)
            pool.sem_inc(sim_read, FREE_SIM)
            pool.sem_inc(exp_done, FREE_EXP)
            pool.sem_inc(pt_done, FREE_PT)
            pool.sem_inc(pv_done, FREE_PV)
            pool.sem_inc(y_done, FREE_Y)
            for bank_free in (pt_evac, o_evac, y_added):
                pool.sem_inc(bank_free, FREE_BANK)

            def build(q, slot, kv):
                for h in range(2):
                    r = slice(64 * h, 64 * h + 64)
                    src = (kz[slot][h] if kv == 0 else v_T)[r, 0:512].rearrange("p (n t) -> p t n", t=CBS)
                    pos = pos_T[r, bass.ds(q, 1), kv].rearrange("p a t -> p (a t)").unsqueeze(2).broadcast_to([64, CBS, NB // 2])
                    c = 32 * kv + 16 * h
                    pool.tensor_tensor(out=kvb[r, :, c:c + NB // 2], in0=src, in1=pos, op=ALU.add).then_inc(bd_ready, 1)
                    pool.wait_ge(bd_ready, q * 4 + (2 * kv + h + 1))

            pool.wait_ge(emptied[0], pro("v0") // 2 + 1)
            pool.wait_ge(emptied[1], pro("pos3") // 2 + 1)
            build(0, 0, 0)
            build(0, 0, 1)
            pool.wait_ge(small_in, 64)
            pool.wait_ge(xn_ready, T)
            b2b = b2_r[:].unsqueeze(1).broadcast_to([P, 2, DIM])
            for m in range(4):
                pool.tensor_tensor(out=acc[:, 2 * m:2 * m + 2], in0=acc[:, 2 * m:2 * m + 2], in1=b2b, op=ALU.add).then_inc(b2_added, 1)
            pool.wait_ge(b2_added, 4)
            pool.wait_ge(filled[1], pro("q1") // 2 + 1)
            split_weights(1, 0, 1)
            for b in range(2):
                pool.wait_ge(filled[b], pro(f"h1_{FT - 2 + b}") // 2 + 1)
            link(pool.memset(kz[1][0][64:128], 0.0))
            link(pool.memset(kz[1][1][0:64], 0.0))
            pool.sem_inc(consts, 1)

            def pair(i, s, prep, split):
                pr = Pair(i, s)

                def scale(b):
                    lo = 0 if b else W
                    pool.wait_ge(r_ready, pr.p * T + (b + 1))
                    pool.tensor_tensor(out=prob[:, b % 4, :, lo:], in0=prob[:, b % 4, :, lo:],
                                       in1=rloc[:, b].unsqueeze(2).broadcast_to([P, 2, 2 * W - lo]), op=ALU.mult).then_inc(p_ready, 1)

                scale(0)
                if prep:
                    pool.wait_ge(conv_done, pr.p + 1)
                    pool.wait_ge(emptied[0], pr.ordinal("k0"))
                    build(pr.p + 1, pr.nxt, 0)
                    pool.wait_ge(emptied[0], pr.ordinal("v0"))
                    build(pr.p + 1, pr.nxt, 1)
                for b in range(1, T):
                    scale(b)
                    if split and b == 2:
                        pool.wait_ge(filled[1], pr.ordinal("q1"))
                    if split and b in (2, 3):
                        split_high(s, i + 1, b - 2)
                    if split and b in (4, 5):
                        split_low(s, pr.p + 2, b - 4)

            with pool.Fori(0, NP // 2 - 1) as i:
                pair(i, 0, True, True)
                pair(i, 1, True, True)
            pair(NP // 2 - 1, 0, True, False)
            pair(NP // 2 - 1, 1, False, False)

        @block.tensor
        def _(pe):
            def item_pro(name, fn):
                k = pro(name)
                if k >= 2:
                    pe.wait_ge(emptied[k % 2], k // 2)
                fn(ring[k % 2]).then_inc(filled[k % 2], 1)

            def tr4(blocks):
                def f(ps):
                    for j, a in enumerate(blocks):
                        w = a.shape[0]
                        last = pe.transpose(ps[:, j * w:(j + 1) * w], a, ident[0:w, 0:w])
                    return last
                return f

            def project(j, half):
                def f(ps):
                    parts = [(w, x, kt) for kt in range(KT) for w, x in ((pw_h, xr_h), (pw_l, xr_h), (pw_h, xr_l))]
                    for n, (w, x, kt) in enumerate(parts):
                        last = pe.matmul(ps[:], w[:, kt, j, :], x[:, kt, half * 512:half * 512 + 512],
                                         start=(n == 0), stop=(n == len(parts) - 1))
                    return last
                return f

            def v_back(half):
                return tr4([v_T[:, (4 * half + j) * P:(4 * half + j + 1) * P] for j in range(4)])

            def conv(slot, t0, t1):
                for t in range(t0, t1):
                    g = 64 * (t % 2)
                    last = pe.matmul(p_conv[g:g + 64, 0:128], kvb[:, t, :],
                                     conv_w[slot][:, :, :, t].rearrange("p a o -> p (a o)"),
                                     start=(t < 2), stop=(t >= CBS - 2), skip_group_check=True)
                return last

            pe.wait_ge(consts, 2)
            for _ in range(WARM):
                pe.matmul(p_y[:, 0:P], ident[:], ident[:], start=True, stop=True)
            for kt in range(KT):
                for half in range(2):
                    if kt == 0:
                        pe.wait_ge(xr_ready, 4 * half + 4)
                    item_pro(f"xr{2 * kt + half}", tr4([xr[:, 4 * half + j, kt * P:kt * P + P] for j in range(4)]))
            pe.wait_ge(pos_in, 32)
            for m in range(4):
                item_pro(f"pos{m}", tr4([pos_raw[:, 8 * m + 2 * j:8 * m + 2 * j + 2, :].rearrange("p h d -> p (h d)") for j in range(4)]))
            pe.wait_ge(w_split, 4)
            for half in range(2):
                pe.wait_ge(x_split[half], KT)
                item_pro(f"k{half}", project(1, half))
            for half in range(2):
                item_pro(f"v{half}", project(2, half))
            pe.wait_ge(wsum, 2)
            pe.matmul(p_y[:, 0:2], ones[:], wstat[:, 0:2], start=True, stop=True).then_inc(wtot, 1)
            pe.wait_ge(xn_ready, T)
            for kt in range(KT):
                for half in range(2):
                    item_pro(f"xn{2 * kt + half}", tr4([xc[:, 4 * half + j, kt * P:kt * P + P] for j in range(4)]))
            for half in range(2):
                item_pro(f"t{half}", v_back(half))
            pe.wait_ge(small_in, 64)
            for g in range(2):
                def f(ps, g=g):
                    for j in range(4):
                        for kt in range(KT):
                            last = pe.matmul(ps[:, j * 96:(j + 1) * 96], xr_T[:, kt, (4 * g + j) * P:(4 * g + j + 1) * P],
                                             wcomb[:, kt], start=(kt == 0), stop=(kt == KT - 1))
                    return last
                item_pro(f"g{g}", f)
            pe.wait_ge(wq_ready, 1)
            for kt in range(KT):
                for half in range(2):
                    item_pro(f"w1{2 * kt + half}", tr4([w1_s[:, 4 * half + j, kt * P:kt * P + P] for j in range(4)]))
            pe.wait_ge(wq_ready, 2)
            for m in range(4):
                item_pro(f"w2{m}", tr4([w2_s[:, e, (2 * m + f) * P:(2 * m + f + 1) * P] for f in range(2) for e in range(2)]))
            for g in range(2):
                for b in range(2):
                    pe.wait_ge(emptied[b], pro(f"w2{2 + b}") // 2 + 1)
                for ft in range(FT):
                    def f(ps, g=g, ft=ft):
                        for kt in range(KT):
                            for x in (xn_h, xn_l):
                                last = pe.matmul(ps[:], w1_T[:, kt, ft * P:(ft + 1) * P], x[:, kt, g * 512:g * 512 + 512],
                                                 start=(kt == 0 and x is xn_h), stop=(kt == KT - 1 and x is xn_l))
                        return last
                    item_pro(f"h{g}_{ft}", f)
                for j in range(2):
                    def f(ps, g=g, j=j):
                        for m in range(2):
                            for ft in range(FT):
                                if j == m == 0:
                                    pe.wait_ge(g_split, FT * g + ft + 1)
                                for x in (g_h, g_l):
                                    last = pe.matmul(ps[:, m * DIM:(m + 1) * DIM], x[:, ft, (2 * j + m) * P:(2 * j + m + 1) * P],
                                                     w2_T[:, ft], start=(ft == 0 and x is g_h), stop=(ft == FT - 1 and x is g_l))
                        return last
                    item_pro(f"f{g}_{j}", f)
            for half in range(2):
                item_pro(f"q{half}", project(0, half))
            pe.wait_ge(bd_ready, 4)
            pe.wait_ge(bd2_ready, 4)
            pe.wait_ge(conv_in[0], 64)
            conv(0, 0, CBS).then_inc(conv_done, 1)

            def sim(p, s, b):
                if b == 1:
                    pe.wait_ge(y_added, p * 4 + FREE_BANK)
                pe.wait_ge(sim_read, p * T + (b + 1))
                lo = (b - 1) * W if b else 0
                for h in range(2):
                    last = pe.matmul(p_sim[b % 2][:, h * 256 + (0 if b else W):(h + 1) * 256], q_T[s][:, b * P:(b + 1) * P],
                                     kz[s][h][:, lo:(b + 1) * W], start=True, stop=True)
                last.then_inc(sim_done, 1)

            def pair(i, s, prep):
                pr = Pair(i, s)
                p, nx = pr.p, pr.nxt

                def item(name, fn):
                    b = int(name[1])
                    ring_wait_free(pe, b, pr.ordinal(name) if prep else pr.ordinal_last(name))
                    fn(ring[b]).then_inc(filled[b], 1)

                def turn_probs(b):
                    pe.wait_ge(p_ready, p * T + (b + 1))
                    pe.wait_ge(pt_evac, p * T + (b + FREE_BANK))
                    for h in range(2):
                        for c in range(0 if b else 1, 2):
                            last = pe.transpose(p_pt[:, (2 * h + c) * P:(2 * h + c + 1) * P],
                                                prob[:, b % 4, h, c * W:(c + 1) * W], ident[:])
                    last.then_inc(pt_done, 1)

                def pv(b):
                    pe.wait_ge(pt_evac, p * T + (b + 1 + FREE_BANK))
                    for c in range(0 if b else 1, 2):
                        for h in range(2):
                            last = pe.matmul(p_o[64 * h:64 * h + 64, (b % 4) * P:(b % 4 + 1) * P],
                                             v_tok[s][:, b - 1 + c, 64 * h:64 * h + 64], prob_T[:, b % 2, 2 * h + c, :],
                                             start=False, stop=True, skip_group_check=True)
                    last.then_inc(pv_done, 1)

                def comp_out(half):
                    pe.wait_ge(emptied[half], pr.ordinal(f"c{half}") if prep else pr.ordinal_last(f"c{half}"))
                    pe.wait_ge(o_evac, p * 2 + (half + FREE_BANK))
                    pe.matmul(p_o[:], cv_bd[:], pc_T[:, half * 512:half * 512 + 512], start=True, stop=False,
                              skip_group_check=True)

                def y(j):
                    half = j // 2
                    if j % 2 == 0:
                        pe.wait_ge(o_evac, p * 2 + (half + 1 + FREE_BANK))
                        pe.wait_ge(outw_in[s], (i + 1) * 16)
                    bank_y = p_y
                    if j < 3:
                        pe.wait_ge(y_added, p * 4 + (j + FREE_BANK))
                    else:
                        pe.wait_ge(sim_read, p * T + (T + FREE_SIM))
                        bank_y = p_sim[1]
                    for m in range(2):
                        c = (2 * (j % 2) + m) * P
                        last = pe.matmul(bank_y[:, m * DIM:(m + 1) * DIM], o_T[:, half, c:c + P], out_w[s][:], start=True, stop=True)
                    last.then_inc(y_done, 1)

                pe.wait_ge(conv_evac, p + 1)
                for h in range(2):
                    pe.matmul(ck_ps[64 * h:64 * h + 64, 16 * h:16 * h + 16], conv_s[:, 0:64], sel[:, 16 * h:16 * h + 16],
                              start=True, stop=True, skip_group_check=True)
                pe.matmul(cv_ps, sel_v[:].rearrange("p a b -> p (a b)"), conv_s[:, 64:128], start=True, stop=True,
                          skip_group_check=True).then_inc(sel_done, 1)
                if prep:
                    pe.wait_ge(w_split, p * 4 + 8)
                    item("k0", project(1, 0))
                    item("k1", project(1, 1))
                pe.wait_ge(ckcv, p + 1)
                pe.wait_ge(pt_evac, p * T + FREE_BANK)
                for g in range(4):
                    last = pe.matmul(p_pt[32 * g:32 * g + 32, 0:256], ck_bd[:], q_T[s][:, g * 256:(g + 1) * 256],
                                     start=True, stop=True, skip_group_check=True)
                last.then_inc(csT_done, 1)
                sim(p, s, 1)
                pe.wait_ge(csT_evac, p + 1)
                for j in range(2):
                    last = pe.transpose(p_conv[:, 256 + j * P:256 + (j + 1) * P], cs_T[:, j * P:(j + 1) * P], ident[:])
                last.then_inc(csim_done, 1)
                if prep:
                    item("v0", project(2, 0))
                    item("v1", project(2, 1))
                if prep:
                    item("q0", project(0, 0))
                    item("q1", project(0, 1))
                turn_probs(0)
                pe.wait_ge(pc_ready, p + 1)
                for half in range(2):
                    def f(ps, half=half):
                        for j in range(4):
                            last = pe.transpose(ps[0:96, j * P:(j + 1) * P],
                                                c_p[:, 4 * half + j].rearrange("p a n -> p (a n)").bitcast(F32), ident[:])
                        return last
                    item(f"c{half}", f)
                sim(p, s, 2)
                comp_out(0)
                for b in range(T):
                    if b:
                        turn_probs(b)
                        if b + 2 < T:
                            sim(p, s, b + 2)
                    if prep:
                        if b == 0:
                            for half in range(2):
                                pe.wait_ge(emptied[half], pr.ordinal(f"v{half}"))
                                item(f"t{half}", v_back(half))
                        else:
                            if b == 1:
                                pe.wait_ge(bd_ready, p * 4 + 8)
                                pe.wait_ge(bd2_ready, p * 4 + 8)
                                pe.wait_ge(conv_in[nx], (pr.nxt_use + 1) * 64)
                                pe.wait_ge(csim_read, p + 1)
                            conv(nx, 8 * (b - 1), 8 * b)
                    if b == 4:
                        comp_out(1)
                    pv(b)
                    if b in (5, 6):
                        y(b - 5)
                if prep:
                    conv(nx, 56, CBS).then_inc(conv_done, 1)
                    sim(p + 1, nx, 0)
                y(2)
                y(3)

            pe.wait_ge(consts, 5)
            for b in range(2):
                pe.wait_ge(emptied[b], pro(f"q{b}") // 2 + 1)
            sim(0, 0, 0)
            with pe.Fori(0, NP // 2 - 1) as i:
                pair(i, 0, True)
                pair(i, 1, True)
            pair(NP // 2 - 1, 0, True)
            pair(NP // 2 - 1, 1, False)

        @block.scalar
        def _(act):
            def item_pro(name):
                k = pro(name)
                assert k % 2 == 0
                act.wait_ge(filled[0], k // 2 + 1)
                return ring[0]

            def take(name, slot, ps):
                if name == "k0":
                    act.copy(kz[slot][0][0:64, 0:512], ps[0:64, :])
                    return act.copy(kz[slot][1][64:128, 0:512], ps[64:128, :])
                if name == "v0":
                    return act.copy(v_T[:, 0:512], ps[:])
                if name == "q0":
                    return act.mul(q_T[slot][:, 0:512], ps[:], SCALE)
                if name == "t0":
                    return act.copy(v_tok[slot][:, 0:4].rearrange("p b n -> p (b n)"), ps[:])
                return act.copy(pc_T[0:96, 0:512], ps[0:96, :])

            def load_table(func):
                act.activation(unused[:, 0:1], unused[:, 1:2], func)

            act.wait_ge(consts, 1)
            load_table(ACT.Sqrt)
            for r in range(2):
                act.wait_ge(rt_in, r + 1)
                act.activation(stat[:, 4 + r], stat[:, 2 + r], ACT.Sqrt).then_inc(rt_out, 1)
            act.wait_ge(rms_in, 16)
            for kt in range(KT):
                ps = item_pro(f"xr{2 * kt}")
                act.activation(xr_T[:, kt, 0:512], ps[:], ACT.Copy, scale=rms_c[:, kt:kt + 1]).then_inc(xr_T_ready, 1)
                act.activation(xr_h[:, kt, 0:512], ps[:], ACT.Copy, scale=rms_c[:, kt:kt + 1]).then_inc(emptied[0], 1)
            for m in range(4):
                wait_filled(act, pro(f"pos{m}"))
                act.copy(pos_T[:, 4 * m:4 * m + 4].rearrange("p a b c -> p (a b c)"), ring[m % 2][:]).then_inc(emptied[m % 2], 1)

            def abs_sums(n, w_s):
                act.wait_ge(w12_in, 32)
                for half in range(2):
                    part = w_s[:, 4 * half:4 * half + 4] if n == 0 else w_s[:, half:half + 1]
                    if n + half:
                        act.wait_ge(wabs, 2 * n + half)
                    act.activation(w_abs.rearrange("p (a b) -> p a b", a=part.shape[1]), part, ACT.Abs,
                                   accum_out=wstat[:, 4 + 2 * n + half:5 + 2 * n + half]).then_inc(wabs, 1)

            act.wait_ge(consts, 3)
            abs_sums(0, w1_s)
            take("k0", 0, item_pro("k0")).then_inc(emptied[0], 1)
            abs_sums(1, w2_s)
            take("v0", 0, item_pro("v0")).then_inc(emptied[0], 1)
            for kt in range(KT):
                for half in range(2):
                    wait_filled(act, pro(f"xn{2 * kt + half}"))
                    act.copy(xn_h[:, kt, 512 * half:512 * half + 512], ring[half][:]).then_inc(xn_h_ready, 1)
            take("t0", 0, item_pro("t0")).then_inc(emptied[0], 1)
            ps = item_pro("g0")
            act.copy(sig[:, 0:4].rearrange("p b n -> p (b n)"), ps[:, 0:384]).then_inc(emptied[0], 1)
            load_table(ACT.Gelu)
            for kt in range(KT):
                act.activation(w1_T[:, kt, 0:512], item_pro(f"w1{2 * kt}")[:], ACT.Copy, bias=-ROUND).then_inc(emptied[0], 1)
            for m in (0, 2):
                act.activation(w2_T[:, 2 * m:2 * m + 2].rearrange("p f e -> p (f e)"), item_pro(f"w2{m}")[:],
                               ACT.Copy, bias=-ROUND).then_inc(emptied[0], 1)
            act.wait_ge(small_in, 64)
            act.wait_ge(bd_ready, 4)
            for g in range(2):
                for ft in range(FT):
                    k = pro(f"h{g}_{ft}")
                    n = FT * g + ft
                    wait_filled(act, k)
                    if n >= 4:
                        act.wait_ge(g_split, n - 3)
                    act.activation(g_f[ft % 4], ring[k % 2][:], ACT.Gelu, bias=b1_c[:, ft:ft + 1]).then_inc(emptied[k % 2], 1)
                    if ft % 2 == 0:
                        act.wait_ge(emptied[0], k // 2 + 1)
                        act.copy(g_h[:, ft], g_f[ft % 4]).then_inc(gh_ready, 1)
            take("q0", 0, item_pro("q0")).then_inc(emptied[0], 1)
            act.wait_ge(glog, 1)
            act.activation(sig[:], sig[:], ACT.Exp, scale=-1.0).then_inc(gexp, 1)

            def exps(p, b):
                lo = 0 if b else W
                act.wait_ge(sim_read, p * T + (b + 1 + FREE_SIM))
                act.wait_ge(pt_done, p * T + (b + 1))
                for h in range(2):
                    act.activation(prob[:, b % 4, h, lo:], s_neg[:, b % 2, h, lo:], ACT.Exp, bias=ncol[:, b, h:h + 1],
                                   scale=-1.0, accum_out=lsum[:, b, h:h + 1]).then_inc(exp_done, 1)

            def pair(i, s, prep):
                pr = Pair(i, s)
                p = pr.p

                def evac(name):
                    act.wait_ge(filled[0], pr.ordinal(name) if prep else pr.ordinal_last(name))
                    take(name, s if name == "c0" else pr.nxt, ring[0]).then_inc(emptied[0], 1)

                def second_half(name):
                    act.wait_ge(filled[1], pr.ordinal(name))
                    if name == "k1":
                        act.wait_ge(bd2_ready, p * 4 + 6)
                        act.copy(kz[pr.nxt][0][0:64, 512:1024], ring[1][0:64, :])
                        last = act.copy(kz[pr.nxt][1][64:128, 512:1024], ring[1][64:128, :])
                    elif name == "v1":
                        last = act.copy(v_T[:, 512:1024], ring[1][:])
                    else:
                        last = act.mul(q_T[pr.nxt][:, 512:1024], ring[1][:], SCALE)
                    last.then_inc(emptied[1], 1)

                if prep:
                    evac("k0")
                act.wait_ge(csT_done, p + 1)
                act.copy(cs_T[:], p_pt[:, 0:256]).then_inc(csT_evac, 1)
                if prep:
                    second_half("k1")
                if prep:
                    evac("v0")
                act.wait_ge(cs_ready, p + 1)
                act.activation(c_e[:], c_s[:], ACT.Exp).then_inc(ce_ready, 1)
                if prep:
                    second_half("v1")
                exps(p, 1)
                if prep:
                    evac("q0")
                    second_half("q1")
                evac("c0")
                for b in range(T):
                    act.wait_ge(pt_done, p * T + (b + 1 + FREE_PT))
                    act.wait_ge(pv_done, p * T + (b - 1 + FREE_PV))
                    turned = p_pt[:].rearrange("p (a n) -> p a n", a=4)
                    which = slice(0, 4) if b else slice(1, 4, 2)
                    act.copy(prob_T[:, b % 2, which], turned[:, which]).then_inc(pt_evac, 1)
                    if b + 2 < T:
                        exps(p, b + 2)
                    if b == 0 and prep:
                        evac("t0")
                if prep:
                    exps(p + 1, 0)

            act.wait_ge(consts, 5)
            exps(0, 0)
            with act.Fori(0, NP // 2 - 1) as i:
                load_table(ACT.Exp)
                pair(i, 0, True)
                pair(i, 1, True)
            pair(NP // 2 - 1, 0, True)
            pair(NP // 2 - 1, 1, False)

        @block.vector
        def _(dve):
            n = [0]

            def link(ins):
                n[0] += 1
                ins.then_inc(dch, 1)
                dve.wait_ge(dch, n[0])

            def item_pro(name):
                k = pro(name)
                dve.wait_ge(filled[k % 2], k // 2 + 1)
                return ring[k % 2]

            for b in range(T):
                if b % 2 == 0:
                    dve.wait_ge(x_in[b // 2], 16)
                last = dve.bn_stats(out=bn[:, b], in_=acc[:, b])
            link(last)
            for b in range(T):
                last = dve.bn_aggr(out=mv[:, b], in_=bn[:, b])
            link(last)
            var = mv[:, :, 1]
            dve.tensor_scalar(stat[:, 2], var, LN_EPS, None, ALU.add).then_inc(rt_in, 1)
            dve.wait_ge(rt_out, 1)
            link(dve.reciprocal(stat[:, 6], stat[:, 4]))
            link(dve.tensor_tensor(out=stat[:, 0], in0=stat[:, 6], in1=stat[:, 6], op=ALU.mult))
            link(dve.tensor_tensor(out=stat[:, 1], in0=stat[:, 0], in1=var, op=ALU.mult))
            dve.tensor_scalar(stat[:, 3], stat[:, 1], RMS_EPS, None, ALU.add).then_inc(rt_in, 1)
            dve.wait_ge(rt_out, 2)
            link(dve.reciprocal(stat[:, 7], stat[:, 5]))
            link(dve.tensor_tensor(out=stat[:, 0], in0=stat[:, 7], in1=stat[:, 6], op=ALU.mult))
            for b in range(T):
                dve.tensor_scalar(xr[:, b], acc[:, b], mv[:, b, 0:1], stat[:, 0, b:b + 1], ALU.subtract, ALU.mult).then_inc(xr_ready, 1)

            def take(name, slot, ps):
                if name == "k1":
                    dve.tensor_copy(kz[slot][0][0:64, 512:1024], ps[0:64, :])
                    return dve.tensor_copy(kz[slot][1][64:128, 512:1024], ps[64:128, :])
                if name == "v1":
                    return dve.tensor_copy(v_T[:, 512:1024], ps[:])
                if name == "q1":
                    return dve.tensor_scalar(q_T[slot][:, 512:1024], ps[:], SCALE, None, ALU.mult)
                if name == "t1":
                    return dve.tensor_copy(v_tok[slot][:, 4:8].rearrange("p b n -> p (b n)"), ps[:])
                return dve.tensor_copy(pc_T[0:96, 512:1024], ps[0:96, :])

            def build(q, kv, ps):
                for h in range(2):
                    r = slice(64 * h, 64 * h + 64)
                    pos = pos_T[r, bass.ds(q, 1), kv].rearrange("p a t -> p (a t)").unsqueeze(2).broadcast_to([64, CBS, NB // 2])
                    c = 32 * kv + 16 * h + NB // 2
                    dve.tensor_tensor(out=kvb[r, :, c:c + NB // 2], in0=ps[r, :].rearrange("p (n t) -> p t n", t=CBS),
                                      in1=pos, op=ALU.add).then_inc(bd2_ready, 1)

            dve.wait_ge(rms_in, 16)
            for kt in range(KT):
                ps = item_pro(f"xr{2 * kt + 1}")
                dve.tensor_scalar(xr_T[:, kt, 512:1024], ps[:], rms_c[:, kt:kt + 1], None, ALU.mult).then_inc(xr_T_ready, 1)
                dve.tensor_scalar(xr_h[:, kt, 512:1024], ps[:], rms_c[:, kt:kt + 1], None, ALU.mult).then_inc(emptied[1], 1)
            dve.wait_ge(xr_T_ready, 4)
            for b in range(2):
                dve.wait_ge(emptied[b], pro(f"xr{2 + b}") // 2 + 1)
            for kt in range(KT):
                dve.tensor_tensor(out=xr_l[:, kt, 0:512], in0=xr_T[:, kt, 0:512], in1=xr_h[:, kt, 0:512],
                                  op=ALU.subtract).then_inc(x_split[0], 1)
            for b in range(T):
                dve.tensor_scalar(xc[:, b], acc[:, b], mv[:, b, 0:1], stat[:, 6, b:b + 1], ALU.subtract, ALU.mult).then_inc(xn_ready, 1)
            dve.wait_ge(consts, 3)
            for half in range(2):
                dve.wait_ge(emptied[half], pro(f"pos{2 + half}") // 2 + 1)

            def prep0(name):
                ps = item_pro(name)
                if name in ("k1", "v1"):
                    build(0, int(name == "v1"), ps)
                take(name, 0, ps).then_inc(emptied[1], 1)

            prep0("k1")
            dve.wait_ge(wabs, 4)
            for j in range(2):
                dve.tensor_tensor(out=wstat[:, j:j + 1], in0=wstat[:, 4 + 2 * j:5 + 2 * j], in1=wstat[:, 5 + 2 * j:6 + 2 * j],
                                  op=ALU.add).then_inc(wsum, 1)
            prep0("v1")
            dve.wait_ge(wtot, 1)
            link(dve.tensor_scalar(wstat[:, 2:4], p_y[:, 0:2], 1.0 / (DFF * DIM), Q_EPS, ALU.mult, ALU.max))
            dve.reciprocal(wstat[:, 8:10], wstat[:, 2:4]).then_inc(wscale, 1)
            for kt in range(KT):
                for half in range(2):
                    ps = item_pro(f"xn{2 * kt + half}")
                    c = slice(512 * half, 512 * half + 512)
                    dve.wait_ge(xn_h_ready, 2 * kt + half + 1)
                    dve.tensor_tensor(out=xn_l[:, kt, c], in0=ps[:], in1=xn_h[:, kt, c], op=ALU.subtract).then_inc(emptied[half], 1)
            def ternary(n_w, w_s):
                dve.wait_ge(wscale, 1)
                link(dve.tensor_scalar(w_s, w_s, wstat[:, 8 + n_w:9 + n_w], 1.0, ALU.mult, ALU.min))
                dve.tensor_scalar(w_s, w_s, -1.0, ROUND, ALU.max, ALU.add).then_inc(wq_ready, 1)

            ternary(0, w1_s)
            prep0("t1")
            ternary(1, w2_s)
            dve.wait_ge(small_in, 64)
            ps = item_pro("g1")
            dve.tensor_copy(sig[:, 4:8].rearrange("p b n -> p (b n)"), ps[:, 0:384]).then_inc(emptied[1], 1)
            for b in range(2):
                dve.wait_ge(emptied[b], pro(f"g{b}") // 2 + 1)
            dve.tensor_tensor(out=sig[:], in0=sig[:], in1=bc_r[:].unsqueeze(1).broadcast_to([P, T, 3 * H]), op=ALU.add).then_inc(glog, 1)
            for kt in range(KT):
                ps = item_pro(f"w1{2 * kt + 1}")
                dve.tensor_scalar(w1_T[:, kt, 512:1024], ps[:], -ROUND, None, ALU.add).then_inc(emptied[1], 1)
            for m in (1, 3):
                ps = item_pro(f"w2{m}")
                dve.tensor_scalar(w2_T[:, 2 * m:2 * m + 2].rearrange("p f e -> p (f e)"), ps[:], -ROUND, None, ALU.add).then_inc(emptied[1], 1)
            dve.wait_ge(b2_added, 4)
            for g in range(2):
                for ft in range(FT):
                    n_h = FT * g + ft
                    dve.wait_ge(emptied[ft % 2], pro(f"h{g}_{ft}") // 2 + 1)
                    if ft % 2:
                        link(dve.tensor_copy(g_h[:, ft], g_f[ft % 4]))
                    else:
                        dve.wait_ge(gh_ready, n_h // 2 + 1)
                    dve.tensor_tensor(out=g_l[:, ft], in0=g_f[ft % 4], in1=g_h[:, ft], op=ALU.subtract).then_inc(g_split, 1)
                for j in range(2):
                    ps = item_pro(f"f{g}_{j}")
                    a = acc[:, 4 * g + 2 * j:4 * g + 2 * j + 2].rearrange("p b c -> p (b c)")
                    dve.tensor_tensor(out=a, in0=a, in1=ps[:], op=ALU.add).then_inc(emptied[pro(f"f{g}_{j}") % 2], 1)

            def conv_out(q, slot, use):
                dve.wait_ge(conv_done, q + 1)
                dve.wait_ge(bias_in[slot], (use + 1) * 64)
                dve.tensor_tensor(out=conv_s[:], in0=p_conv[:, 0:128], in1=conv_b[slot][:], op=ALU.add).then_inc(conv_evac, 1)

            prep0("q1")
            dve.wait_ge(gexp, 1)
            link(dve.tensor_scalar(sig[:], sig[:], 1.0, None, ALU.add))
            link(dve.reciprocal(sig[:], sig[:]))
            sg = sig[:].rearrange("p b (q h k) -> p q b h k", h=2, k=3)
            dve.tensor_tensor(out=gate[:, :, 0], in0=sg[:, :, :, :, 0], in1=sg[:, :, :, :, 1], op=ALU.add).then_inc(gates, 1)
            dve.tensor_copy(gate[:, :, 1], sg[:, :, :, :, 2]).then_inc(gates, 1)
            conv_out(0, 0, 0)
            dve.wait_ge(gates, 2)

            CCHAIN, LCHAIN = 9, 8

            def scores(p, b):
                c0 = 0 if b else 1
                dve.wait_ge(sim_done, p * T + (b + 1))
                dve.wait_ge(exp_done, (p * T + b) * 2 + 2)
                dve.sem_inc(step_begun, 1)
                for h in range(2):
                    ins = dve.tensor_tensor_reduce(
                        out=s_neg[:, b % 2, h, c0 * W:].rearrange("p (c j) -> p c j", j=W),
                        in0=p_sim[b % 2][:, h * 256 + c0 * W:(h + 1) * 256].rearrange("p (c j) -> p c j", j=W),
                        in1=mask_l[:, c0:], scale=-1.0, scalar=-NEG * 2, op0=ALU.add, op1=ALU.min,
                        accum_out=ncol[:, b, h:h + 1])
                ins.then_inc(sim_read, 1)

            def pair(i, s, prep):
                pr = Pair(i, s)
                p = pr.p
                c, l = [0], [0]

                def link_c(ins):
                    c[0] += 1
                    ins.then_inc(cchain, 1)
                    dve.wait_ge(cchain, p * CCHAIN + c[0])

                def build_half(name):
                    if name == "k1":
                        dve.wait_ge(filled[1], pr.ordinal(name))
                        build(p + 1, 0, ring[1])
                    else:
                        dve.wait_ge(emptied[1], pr.ordinal(name))
                        build(p + 1, 1, v_T[:, 512:1024])

                def evac(name):
                    dve.wait_ge(filled[1], pr.ordinal(name) if prep else pr.ordinal_last(name))
                    take(name, s if name == "c1" else pr.nxt, ring[1]).then_inc(emptied[1], 1)

                def row_scale(b):
                    l[0] += 1
                    dve.wait_ge(exp_done, (p * T + b) * 2 + (2 + FREE_EXP))
                    dve.reciprocal(rinv[:, b], lsum[:, b]).then_inc(lchain, 1)
                    dve.wait_ge(lchain, p * LCHAIN + l[0])
                    dve.tensor_tensor(out=rloc[:, b], in0=rinv[:, b], in1=gate_p[:, 0, b], op=ALU.mult).then_inc(r_ready, 1)

                def y_add(j):
                    dve.wait_ge(y_done, p * 4 + (j + 1 + FREE_Y))
                    dve.wait_ge(y_added, p * 4 + (j + FREE_BANK))
                    a = acc[:, 2 * j:2 * j + 2].rearrange("p b c -> p (b c)")
                    dve.tensor_tensor(out=a, in0=a, in1=(p_y if j < 3 else p_sim[1])[:], op=ALU.add).then_inc(y_added, 1)

                def o_out(half):
                    dve.wait_ge(pv_done, p * T + (4 * half + 4 + FREE_PV))
                    dve.wait_ge(y_done, p * 4 + (2 * half - 2 + FREE_Y))
                    dve.tensor_copy(o_T[:, half], p_o[:]).then_inc(o_evac, 1)

                dve.wait_ge(sel_done, p + 1)
                for h in range(2):
                    dve.tensor_copy(ck_bd[64 * h:64 * h + 64, 16 * h:16 * h + 16], ck_ps[64 * h:64 * h + 64, 16 * h:16 * h + 16])
                link_c(dve.tensor_tensor(out=cv_f[0:96].rearrange("p (h o) -> p h o", h=2), in0=cv_ps.unsqueeze(1).broadcast_to([96, 2, DH]),
                                         in1=block_m[0:96], op=ALU.mult))
                link_c(dve.tensor_copy(cv_bd[0:96], cv_f[0:96]))
                dve.tensor_tensor(out=cv_bd[64:96], in0=cv_f[64:96], in1=cv_bd[64:96], op=ALU.subtract).then_inc(ckcv, 1)
                link_c(dve.tensor_copy(gate_p[:].rearrange("p a b c -> p (a b c)"), gate[:, bass.ds(p, 1)].rearrange("p q a b c -> p (q a b c)")))
                row_scale(0)
                if prep:
                    build_half("k1")
                scores(p, 1)
                dve.wait_ge(csim_done, p + 1)
                dve.tensor_tensor(out=c_s[:], in0=csim_ps, in1=mask_c[:].unsqueeze(2).broadcast_to([P, T, 2, NB]), op=ALU.add).then_inc(csim_read, 1)
                dve.wait_ge(csim_read, p + 1)
                cs2 = c_s[:].rearrange("p b h n -> p (b h) n")
                link_c(dve.tensor_reduce(c_m[:], cs2, AX.X, ALU.max))
                dve.tensor_tensor(out=cs2, in0=cs2, in1=c_m[:].unsqueeze(2).broadcast_to([P, 2 * T, NB]), op=ALU.subtract).then_inc(cs_ready, 1)
                dve.wait_ge(ce_ready, p + 1)
                ce2 = c_e[:].rearrange("p b h n -> p (b h) n")
                link_c(dve.tensor_reduce(c_l[:], ce2, AX.X, ALU.add))
                link_c(dve.reciprocal(c_r[:], c_l[:]))
                link_c(dve.tensor_tensor(out=c_g[:], in0=c_r[:], in1=gate_p[:, 1].rearrange("p b h -> p (b h)"), op=ALU.mult))
                link_c(dve.tensor_tensor(out=c_f[:].rearrange("p b (h n) -> p (b h) n", h=2), in0=ce2,
                                         in1=c_g[:].unsqueeze(2).broadcast_to([P, 2 * T, NB]), op=ALU.mult))
                link_c(dve.tensor_copy(c_p[:, :, 0:3:2], c_f[:].unsqueeze(2).broadcast_to([P, T, 2, 2 * NB])))
                dve.tensor_tensor(out=c_p[:, :, 1], in0=c_f[:], in1=c_p[:, :, 0], op=ALU.subtract).then_inc(pc_ready, 1)
                if prep:
                    build_half("v1")
                row_scale(1)
                evac("c1")
                for b in range(T):
                    if b == 4:
                        o_out(0)
                    if b + 2 < T:
                        scores(p, b + 2)
                        row_scale(b + 2)
                    if b == 0 and prep:
                        evac("t1")
                    if b in (6, 7):
                        y_add(b - 6)
                o_out(1)
                if prep:
                    conv_out(p + 1, pr.nxt, pr.nxt_use)
                    scores(p + 1, 0)
                y_add(2)
                y_add(3)
                assert c[0] == CCHAIN and l[0] == LCHAIN, (c, l)

            dve.wait_ge(consts, 5)
            scores(0, 0)
            with dve.Fori(0, NP // 2 - 1) as i:
                pair(i, 0, True)
                pair(i, 1, True)
            pair(NP // 2 - 1, 0, True)
            pair(NP // 2 - 1, 1, False)


_INS = ["L0_attn_inp", "L0_attn_rms_w", "L0_attn_w_qkv", "L0_attn_k_pos", "L0_attn_v_pos", "L0_attn_kc_w",
        "L0_attn_kc_b", "L0_attn_vc_w", "L0_attn_vc_b", "L0_attn_w_comb", "L0_attn_b_comb", "L0_attn_w_out",
        "L0_ffn_w1", "L0_ffn_b1", "L0_ffn_w2", "L0_ffn_b2"]


def kernel(**inputs):
    import numpy as _np
    import concourse.bacc as _bacc
    from concourse import mybir as _mybir
    from concourse.bass_utils import run_bass_kernel_spmd as _run

    nc = _bacc.Bacc("TRN2", target_bir_lowering=False, num_devices=1)
    arrays, args = {}, []
    for name in _INS:
        a = _np.ascontiguousarray(inputs[name])
        arrays[f"in_{name}_dram"] = a
        args.append(nc.dram_tensor(f"in_{name}_dram", a.shape, _mybir.dt.from_np(a.dtype), kind="ExternalInput").ap())
    args.append(nc.dram_tensor("out_0_dram", (1, S, DIM), F32, kind="ExternalOutput").ap())
    layer(nc, *args)
    r = _run(nc, [arrays], core_ids=[0])
    return r.results[0]["out_0_dram"]
```
